# Optimizing a Trainium2 kernel written in Bass

```python
import numpy as np
import jax
import jax.numpy as jnp

def _softmax(x, axis=-1):
    return jax.nn.softmax(x, axis=axis)

def _gelu(x):
    return jax.nn.gelu(x, approximate=True)

def _silu(x):
    return jax.nn.silu(x)

def _sigmoid(x):
    return jax.nn.sigmoid(x)

def _layernorm(x, axis=-1, eps=1e-05):
    m = jnp.mean(x, axis=axis, keepdims=True)
    v = jnp.var(x, axis=axis, keepdims=True)
    return (x - m) / jnp.sqrt(v + eps)

def _scatter_add(tgt, idx, src, axis=0):
    return tgt.at[idx].add(src)

def _segment_sum(src, seg, n):
    return jax.ops.segment_sum(src, seg, n)
kernel_name = 'mk_early_fusion_d2_tok_img256_r4_1a2104'

def setup_inputs(seed: int=0):
    np.random.seed(seed)
    _w = jnp.asarray

    def _rec_inputs():
        import jax
        import jax.numpy as jnp
        _rk = jax.random.key(seed)
        x = -7.10856e-05 + 0.999911 * jax.random.normal(jax.random.fold_in(_rk, 1), (128, 1, 224, 224), jnp.float32)
        txt = 7.83249e-05 + 0.02 * jax.random.normal(jax.random.fold_in(_rk, 2), (128, 32, 64), jnp.float32)
        return (x, txt)
    x, txt = _rec_inputs()

    def _L0_tok_setup():
        import jax, jax.numpy as jnp
        import numpy as np
        INV_SQRT2 = 0.7071067811865476

        def haar_dwt2(x):
            lo = (x[..., ::2] + x[..., 1::2]) * INV_SQRT2
            hi = (x[..., ::2] - x[..., 1::2]) * INV_SQRT2
            cA = (lo[..., ::2, :] + lo[..., 1::2, :]) * INV_SQRT2
            cH = (lo[..., ::2, :] - lo[..., 1::2, :]) * INV_SQRT2
            cV = (hi[..., ::2, :] + hi[..., 1::2, :]) * INV_SQRT2
            cD = (hi[..., ::2, :] - hi[..., 1::2, :]) * INV_SQRT2
            return (cA, (cH, cV, cD))

        def wavedec2_maps(x, levels):
            a = x
            details = []
            for _ in range(levels):
                a, d = haar_dwt2(a)
                details.append(d)
            maps = [a]
            for d in reversed(details):
                maps.extend(d)
            return maps
        key = jax.random.key(seed)
        k1, k2 = jax.random.split(key)
        B, H, W_img = (64, 256, 256)
        x = jax.random.normal(k1, (B, 1, H, W_img), dtype=jnp.float32)
        n_maps = 1 + 3 * 2
        W = jax.random.normal(k2, (n_maps, 64), dtype=jnp.float32) * (1.0 / np.sqrt(n_maps))
        b = jnp.zeros((64,), dtype=jnp.float32)
        return {'x': x, 'W': W, 'b': b}
    _L0_tok_all = _L0_tok_setup()
    _L0_tok_in = {k: v for k, v in _L0_tok_all.items() if k in ('W', 'b')}
    del _L0_tok_all

    def _L0_attn_setup():
        import jax, jax.numpy as jnp
        import numpy as np
        D, S, E, MPE = (64, 128, 128, 1024)
        B, N = (2, 1024)

        def _rope(x):
            n, d = (x.shape[-2], x.shape[-1])
            half = d // 2
            pos = jnp.arange(n, dtype=x.dtype)
            inv_freq = 10000.0 ** (-jnp.arange(half, dtype=x.dtype) / half)
            sinusoid = pos[:, None] * inv_freq
            sin, cos = (jnp.sin(sinusoid), jnp.cos(sinusoid))
            x1, x2 = jnp.split(x, 2, axis=-1)
            return jnp.concatenate([x1 * cos - x2 * sin, x2 * cos + x1 * sin], axis=-1)
        key = jax.random.key(seed)
        ks = jax.random.split(key, 12)
        std = 0.02
        return {'query': jax.random.normal(ks[0], (B, N, D), jnp.float32), 'ln_w': jnp.ones((D,), jnp.float32), 'ln_b': jnp.zeros((D,), jnp.float32), 'Wu': jax.random.normal(ks[1], (D, E), jnp.float32) / np.float32(np.sqrt(D)), 'bu': jnp.zeros((E,), jnp.float32), 'Wv': jax.random.normal(ks[2], (D, E), jnp.float32) / np.float32(np.sqrt(D)), 'bv': jnp.zeros((E,), jnp.float32), 'Wbase': jax.random.normal(ks[3], (D, S), jnp.float32) / np.float32(np.sqrt(D)), 'bbase': jnp.zeros((S,), jnp.float32), 'q_w': jax.random.normal(ks[4], (1, S), jnp.float32) * std, 'q_b': jnp.zeros((1, S), jnp.float32), 'k_w': jax.random.normal(ks[5], (1, S), jnp.float32) * std, 'k_b': jnp.zeros((1, S), jnp.float32), 'w_rel': jax.random.normal(ks[6], (2 * MPE - 1,), jnp.float32) * std, 'Wo': jax.random.normal(ks[7], (E, D), jnp.float32) / np.float32(np.sqrt(E)), 'bo': jnp.zeros((D,), jnp.float32)}
    _L0_attn_all = _L0_attn_setup()
    _L0_attn_in = {k: v for k, v in _L0_attn_all.items() if k in ('ln_w', 'ln_b', 'Wu', 'bu', 'Wv', 'bv', 'Wbase', 'bbase', 'q_w', 'q_b', 'k_w', 'k_b', 'w_rel', 'Wo', 'bo')}
    del _L0_attn_all

    def _L0_ffn_setup():
        import jax, jax.numpy as jnp
        import numpy as np
        B, S, H, NH, NE = (4, 256, 64, 4, 4)
        D = H // NH
        EPS = 1e-08

        def layernorm(x, g, b):
            m = jnp.mean(x, axis=-1, keepdims=True)
            v = jnp.mean((x - m) ** 2, axis=-1, keepdims=True)
            return (x - m) / jnp.sqrt(v + EPS) * g + b
        key = jax.random.key(seed)
        ks = jax.random.split(key, 18)
        sc = 0.05
        return {'x': jax.random.normal(ks[0], (B, S, H), jnp.float32), 'hl_w': jax.random.normal(ks[1], (NH, D, H), jnp.float32) * sc, 'hl_b': jax.random.normal(ks[2], (NH, D), jnp.float32) * sc, 'wq': jax.random.normal(ks[3], (NH, NE, D, D), jnp.float32) * sc, 'wk': jax.random.normal(ks[4], (NH, D, D), jnp.float32) * sc, 'wv': jax.random.normal(ks[5], (NH, D, D), jnp.float32) * sc, 'gate_w': jax.random.normal(ks[6], (NH, NE, NE * D), jnp.float32) * sc, 'gate_b': jax.random.normal(ks[7], (NH, NE), jnp.float32) * sc, 'ln_g': jnp.ones((D,), jnp.float32), 'ln_b': jnp.zeros((D,), jnp.float32), 'fc1_w': jax.random.normal(ks[8], (D, D), jnp.float32) * sc, 'fc1_b': jax.random.normal(ks[9], (D,), jnp.float32) * sc, 'fc2_w': jax.random.normal(ks[10], (D, D), jnp.float32) * sc, 'fc2_b': jax.random.normal(ks[11], (D,), jnp.float32) * sc, 'fnorm_g': jnp.ones((D,), jnp.float32), 'fnorm_b': jnp.zeros((D,), jnp.float32), 'fgate_w': jax.random.normal(ks[12], (NH, H), jnp.float32) * sc}
    _L0_ffn_all = _L0_ffn_setup()
    _L0_ffn_in = {k: v for k, v in _L0_ffn_all.items() if k in ('hl_w', 'hl_b', 'wq', 'wk', 'wv', 'gate_w', 'gate_b', 'ln_g', 'ln_b', 'fc1_w', 'fc1_b', 'fc2_w', 'fc2_b', 'fnorm_g', 'fnorm_b', 'fgate_w')}
    del _L0_ffn_all

    def _L1_attn_setup():
        import jax, jax.numpy as jnp
        import numpy as np
        B, T, C, HR = (8, 1024, 64, 4)
        N_LAYER, LAYER_ID = (12, 3)
        HID = HR * C

        def _fancy_decay_first():
            r01 = LAYER_ID / (N_LAYER - 1)
            h = np.arange(C, dtype=np.float32)
            decay = -5.0 + 8.0 * (h / (C - 1)) ** (0.7 + 1.3 * r01)
            zig = (np.arange(1, C + 1) % 3 - 1).astype(np.float32) * 0.5
            first = np.float32(np.log(0.3)) + zig
            return (jnp.asarray(decay, jnp.float32), jnp.asarray(first, jnp.float32))

        def _ln(x, g, b):
            m = jnp.mean(x, axis=-1, keepdims=True)
            v = jnp.var(x, axis=-1, keepdims=True)
            return (x - m) * jax.lax.rsqrt(v + 1e-05) * g + b

        def _wkv(w, u, k, v):
            Bb, Tt, Cc = k.shape
            kT = jnp.swapaxes(k, 0, 1)
            vT = jnp.swapaxes(v, 0, 1)

            def step(carry, kv):
                p, q, o = carry
                kt, vt = kv
                no = jnp.maximum(o, u + kt)
                A = jnp.exp(o - no)
                E = jnp.exp(u + kt - no)
                y = (A * p + E * vt) / (A * q + E)
                no2 = jnp.maximum(w + o, kt)
                A2 = jnp.exp(w + o - no2)
                E2 = jnp.exp(kt - no2)
                return ((A2 * p + E2 * vt, A2 * q + E2, no2), y)
            init = (jnp.zeros((Bb, Cc), k.dtype), jnp.zeros((Bb, Cc), k.dtype), jnp.full((Bb, Cc), -1e+38, k.dtype))
            _, yT = jax.lax.scan(step, init, (kT, vT))
            return jnp.swapaxes(yT, 0, 1)
        key = jax.random.key(seed)
        ks = jax.random.split(key, 12)
        s = 0.02
        decay, first = _fancy_decay_first()
        return {'x': jax.random.normal(ks[0], (B, T, C), jnp.float32), 'Wk': jax.random.normal(ks[1], (C, C), jnp.float32) * s, 'Wv': jax.random.normal(ks[2], (C, C), jnp.float32) * s, 'Wr': jax.random.normal(ks[3], (C, C), jnp.float32) * s, 'Wo': jax.random.normal(ks[4], (C, C), jnp.float32) * s, 'Wk_ffn': jax.random.normal(ks[5], (C, HID), jnp.float32) * s, 'Wv_ffn': jax.random.normal(ks[6], (HID, C), jnp.float32) * s, 'Wr_ffn': jax.random.normal(ks[7], (C, C), jnp.float32) * s, 'g1': 1.0 + 0.1 * jax.random.normal(ks[8], (C,), jnp.float32), 'b1': 0.1 * jax.random.normal(ks[9], (C,), jnp.float32), 'g2': 1.0 + 0.1 * jax.random.normal(ks[10], (C,), jnp.float32), 'b2': 0.1 * jax.random.normal(ks[11], (C,), jnp.float32), 'spatial_decay': decay, 'spatial_first': first}
    _L1_attn_all = _L1_attn_setup()
    _L1_attn_in = {k: v for k, v in _L1_attn_all.items() if k in ('Wk', 'Wv', 'Wr', 'Wo', 'Wk_ffn', 'Wv_ffn', 'Wr_ffn', 'g1', 'b1', 'g2', 'b2', 'spatial_decay', 'spatial_first')}
    del _L1_attn_all

    def _L1_ffn_setup():
        import jax, jax.numpy as jnp
        import numpy as np
        D_IN, D_HID, D_OUT = (64, 128, 64)
        N_EXPERTS, TOP_K = (64, 2)
        B, S = (8, 1024)
        key = jax.random.key(seed)
        ks = jax.random.split(key, 8)
        scale_in = 1.0 / np.sqrt(D_IN)
        scale_hid = 1.0 / np.sqrt(D_HID)
        return {'x': jax.random.normal(ks[0], (B, S, D_IN), dtype=jnp.float32), 'Wr': jax.random.uniform(ks[1], (D_IN, N_EXPERTS), jnp.float32, -scale_in, scale_in), 'br': jax.random.uniform(ks[2], (N_EXPERTS,), jnp.float32, -scale_in, scale_in), 'W1': jax.random.uniform(ks[3], (N_EXPERTS, D_IN, D_HID), jnp.float32, -scale_in, scale_in), 'b1': jax.random.uniform(ks[4], (N_EXPERTS, D_HID), jnp.float32, -scale_in, scale_in), 'W2': jax.random.uniform(ks[5], (N_EXPERTS, D_HID, D_OUT), jnp.float32, -scale_hid, scale_hid), 'b2': jax.random.uniform(ks[6], (N_EXPERTS, D_OUT), jnp.float32, -scale_hid, scale_hid)}
    _L1_ffn_all = _L1_ffn_setup()
    _L1_ffn_in = {k: v for k, v in _L1_ffn_all.items() if k in ('Wr', 'br', 'W1', 'b1', 'W2', 'b2')}
    del _L1_ffn_all
    return {'x': x, 'txt': txt, 'L0_tok_W': _L0_tok_in['W'], 'L0_tok_b': _L0_tok_in['b'], 'L0_attn_ln_w': _L0_attn_in['ln_w'], 'L0_attn_ln_b': _L0_attn_in['ln_b'], 'L0_attn_Wu': _L0_attn_in['Wu'], 'L0_attn_bu': _L0_attn_in['bu'], 'L0_attn_Wv': _L0_attn_in['Wv'], 'L0_attn_bv': _L0_attn_in['bv'], 'L0_attn_Wbase': _L0_attn_in['Wbase'], 'L0_attn_bbase': _L0_attn_in['bbase'], 'L0_attn_q_w': _L0_attn_in['q_w'], 'L0_attn_q_b': _L0_attn_in['q_b'], 'L0_attn_k_w': _L0_attn_in['k_w'], 'L0_attn_k_b': _L0_attn_in['k_b'], 'L0_attn_w_rel': _L0_attn_in['w_rel'], 'L0_attn_Wo': _L0_attn_in['Wo'], 'L0_attn_bo': _L0_attn_in['bo'], 'L0_ffn_hl_w': _L0_ffn_in['hl_w'], 'L0_ffn_hl_b': _L0_ffn_in['hl_b'], 'L0_ffn_wq': _L0_ffn_in['wq'], 'L0_ffn_wk': _L0_ffn_in['wk'], 'L0_ffn_wv': _L0_ffn_in['wv'], 'L0_ffn_gate_w': _L0_ffn_in['gate_w'], 'L0_ffn_gate_b': _L0_ffn_in['gate_b'], 'L0_ffn_ln_g': _L0_ffn_in['ln_g'], 'L0_ffn_ln_b': _L0_ffn_in['ln_b'], 'L0_ffn_fc1_w': _L0_ffn_in['fc1_w'], 'L0_ffn_fc1_b': _L0_ffn_in['fc1_b'], 'L0_ffn_fc2_w': _L0_ffn_in['fc2_w'], 'L0_ffn_fc2_b': _L0_ffn_in['fc2_b'], 'L0_ffn_fnorm_g': _L0_ffn_in['fnorm_g'], 'L0_ffn_fnorm_b': _L0_ffn_in['fnorm_b'], 'L0_ffn_fgate_w': _L0_ffn_in['fgate_w'], 'L1_attn_Wk': _L1_attn_in['Wk'], 'L1_attn_Wv': _L1_attn_in['Wv'], 'L1_attn_Wr': _L1_attn_in['Wr'], 'L1_attn_Wo': _L1_attn_in['Wo'], 'L1_attn_Wk_ffn': _L1_attn_in['Wk_ffn'], 'L1_attn_Wv_ffn': _L1_attn_in['Wv_ffn'], 'L1_attn_Wr_ffn': _L1_attn_in['Wr_ffn'], 'L1_attn_g1': _L1_attn_in['g1'], 'L1_attn_b1': _L1_attn_in['b1'], 'L1_attn_g2': _L1_attn_in['g2'], 'L1_attn_b2': _L1_attn_in['b2'], 'L1_attn_spatial_decay': _L1_attn_in['spatial_decay'], 'L1_attn_spatial_first': _L1_attn_in['spatial_first'], 'L1_ffn_Wr': _L1_ffn_in['Wr'], 'L1_ffn_br': _L1_ffn_in['br'], 'L1_ffn_W1': _L1_ffn_in['W1'], 'L1_ffn_b1': _L1_ffn_in['b1'], 'L1_ffn_W2': _L1_ffn_in['W2'], 'L1_ffn_b2': _L1_ffn_in['b2']}

def reference(x, txt, L0_tok_W, L0_tok_b, L0_attn_ln_w, L0_attn_ln_b, L0_attn_Wu, L0_attn_bu, L0_attn_Wv, L0_attn_bv, L0_attn_Wbase, L0_attn_bbase, L0_attn_q_w, L0_attn_q_b, L0_attn_k_w, L0_attn_k_b, L0_attn_w_rel, L0_attn_Wo, L0_attn_bo, L0_ffn_hl_w, L0_ffn_hl_b, L0_ffn_wq, L0_ffn_wk, L0_ffn_wv, L0_ffn_gate_w, L0_ffn_gate_b, L0_ffn_ln_g, L0_ffn_ln_b, L0_ffn_fc1_w, L0_ffn_fc1_b, L0_ffn_fc2_w, L0_ffn_fc2_b, L0_ffn_fnorm_g, L0_ffn_fnorm_b, L0_ffn_fgate_w, L1_attn_Wk, L1_attn_Wv, L1_attn_Wr, L1_attn_Wo, L1_attn_Wk_ffn, L1_attn_Wv_ffn, L1_attn_Wr_ffn, L1_attn_g1, L1_attn_b1, L1_attn_g2, L1_attn_b2, L1_attn_spatial_decay, L1_attn_spatial_first, L1_ffn_Wr, L1_ffn_br, L1_ffn_W1, L1_ffn_b1, L1_ffn_W2, L1_ffn_b2):
    import jax
    import jax.numpy as jnp

    def _L0_tok_ref(x, W, b):
        import jax, jax.numpy as jnp
        import numpy as np
        INV_SQRT2 = 0.7071067811865476

        def haar_dwt2(x):
            lo = (x[..., ::2] + x[..., 1::2]) * INV_SQRT2
            hi = (x[..., ::2] - x[..., 1::2]) * INV_SQRT2
            cA = (lo[..., ::2, :] + lo[..., 1::2, :]) * INV_SQRT2
            cH = (lo[..., ::2, :] - lo[..., 1::2, :]) * INV_SQRT2
            cV = (hi[..., ::2, :] + hi[..., 1::2, :]) * INV_SQRT2
            cD = (hi[..., ::2, :] - hi[..., 1::2, :]) * INV_SQRT2
            return (cA, (cH, cV, cD))

        def wavedec2_maps(x, levels):
            a = x
            details = []
            for _ in range(levels):
                a, d = haar_dwt2(a)
                details.append(d)
            maps = [a]
            for d in reversed(details):
                maps.extend(d)
            return maps
        imgs = x[:, 0]
        B = imgs.shape[0]
        maps = wavedec2_maps(imgs, 2)
        proc = [jax.image.resize(m, (B, 8, 8), method='bilinear') for m in maps]
        feat = jnp.stack(proc, axis=1)
        feat = feat.reshape(B, feat.shape[1], 64).transpose(0, 2, 1)
        return feat @ W + b

    def _L0_attn_ref(query, ln_w, ln_b, Wu, bu, Wv, bv, Wbase, bbase, q_w, q_b, k_w, k_b, w_rel, Wo, bo):
        import jax, jax.numpy as jnp
        import numpy as np
        D, S, E, MPE = (64, 128, 128, 1024)
        B, N = (2, 1024)

        def _rope(x):
            n, d = (x.shape[-2], x.shape[-1])
            half = d // 2
            pos = jnp.arange(n, dtype=x.dtype)
            inv_freq = 10000.0 ** (-jnp.arange(half, dtype=x.dtype) / half)
            sinusoid = pos[:, None] * inv_freq
            sin, cos = (jnp.sin(sinusoid), jnp.cos(sinusoid))
            x1, x2 = jnp.split(x, 2, axis=-1)
            return jnp.concatenate([x1 * cos - x2 * sin, x2 * cos + x1 * sin], axis=-1)
        mpe = (w_rel.shape[0] + 1) // 2
        bsz, n, d = query.shape
        mu = query.mean(axis=-1, keepdims=True)
        var = ((query - mu) ** 2).mean(axis=-1, keepdims=True)
        x = (query - mu) * jax.lax.rsqrt(var + 1e-05) * ln_w + ln_b
        u = jax.nn.silu(x @ Wu + bu)
        v = jax.nn.silu(x @ Wv + bv)
        base = jax.nn.silu(x @ Wbase + bbase)
        q = _rope(base * q_w + q_b)
        k = _rope(base * k_w + k_b)
        qk = jnp.einsum('bms,bns->bmn', q, k)
        i = jnp.arange(n)
        bias = w_rel[mpe - 1 + i[None, :] - i[:, None]]
        kernel = jnp.square(jax.nn.relu(qk / mpe + bias))
        out = u * jnp.einsum('bmn,bne->bme', kernel, v) @ Wo + bo
        return out

    def _L0_ffn_ref(x, hl_w, hl_b, wq, wk, wv, gate_w, gate_b, ln_g, ln_b, fc1_w, fc1_b, fc2_w, fc2_b, fnorm_g, fnorm_b, fgate_w):
        import jax, jax.numpy as jnp
        import numpy as np
        B, S, H, NH, NE = (4, 256, 64, 4, 4)
        D = H // NH
        EPS = 1e-08

        def layernorm(x, g, b):
            m = jnp.mean(x, axis=-1, keepdims=True)
            v = jnp.mean((x - m) ** 2, axis=-1, keepdims=True)
            return (x - m) / jnp.sqrt(v + EPS) * g + b
        b, s, h = x.shape
        nh, d, _ = wk.shape
        ne = wq.shape[1]
        sx = jnp.einsum('bsh,ndh->bnsd', x, hl_w) + hl_b[None, :, None, :]
        pad = sx == 0
        q = jnp.einsum('bnsd,neod->bneso', sx, wq)
        k = jnp.einsum('bnsd,nod->bnso', sx, wk)
        v = jnp.einsum('bnsd,nod->bnso', sx, wv)
        causal = jnp.where(jnp.tril(jnp.ones((s, s), bool)), 0.0, -jnp.inf).astype(x.dtype)
        scores = jnp.einsum('bnesd,bntd->bnest', q, k) * d ** 0.5 + causal
        att = jax.nn.softmax(scores, axis=-1)
        qkv = jnp.einsum('bnest,bntd->bnesd', att, v)
        qkv = jnp.where(pad[:, :, None], 0.0, qkv)
        out = jnp.transpose(qkv, (0, 1, 3, 2, 4)).reshape(b, nh, s, ne * d)
        gs = jax.nn.softmax(jnp.einsum('bnsf,nef->bnse', out, gate_w) + gate_b[None, :, None, :], axis=-1)
        mixed = jnp.einsum('bnsed,bnse->bnsd', out.reshape(b, nh, s, ne, d), gs)
        resid = sx[jnp.arange(nh), jnp.arange(nh)]
        hn = layernorm(mixed + resid, ln_g, ln_b)
        f_n = jnp.transpose(hn, (0, 2, 1, 3)).reshape(b, s, h)
        fx = f_n.reshape(b, s, nh, d)
        pm = fx == 0
        hx = jnp.where(pm, 0.0, fx @ fc1_w.T + fc1_b)
        hx = jax.nn.relu(hx)
        hx = jnp.where(pm, 0.0, hx @ fc2_w.T + fc2_b)
        hx = layernorm(hx + fx, fnorm_g, fnorm_b)
        fout = hx.reshape(b, s, h)
        fg = jax.nn.softmax(fout @ fgate_w.T, axis=-1)
        return (fout.reshape(b, s, nh, d) * fg[..., None]).reshape(b, s, h)

    def _L1_attn_ref(x, Wk, Wv, Wr, Wo, Wk_ffn, Wv_ffn, Wr_ffn, g1, b1, g2, b2, spatial_decay, spatial_first):
        import jax, jax.numpy as jnp
        import numpy as np
        B, T, C, HR = (8, 1024, 64, 4)
        N_LAYER, LAYER_ID = (12, 3)
        HID = HR * C

        def _fancy_decay_first():
            r01 = LAYER_ID / (N_LAYER - 1)
            h = np.arange(C, dtype=np.float32)
            decay = -5.0 + 8.0 * (h / (C - 1)) ** (0.7 + 1.3 * r01)
            zig = (np.arange(1, C + 1) % 3 - 1).astype(np.float32) * 0.5
            first = np.float32(np.log(0.3)) + zig
            return (jnp.asarray(decay, jnp.float32), jnp.asarray(first, jnp.float32))

        def _ln(x, g, b):
            m = jnp.mean(x, axis=-1, keepdims=True)
            v = jnp.var(x, axis=-1, keepdims=True)
            return (x - m) * jax.lax.rsqrt(v + 1e-05) * g + b

        def _wkv(w, u, k, v):
            Bb, Tt, Cc = k.shape
            kT = jnp.swapaxes(k, 0, 1)
            vT = jnp.swapaxes(v, 0, 1)

            def step(carry, kv):
                p, q, o = carry
                kt, vt = kv
                no = jnp.maximum(o, u + kt)
                A = jnp.exp(o - no)
                E = jnp.exp(u + kt - no)
                y = (A * p + E * vt) / (A * q + E)
                no2 = jnp.maximum(w + o, kt)
                A2 = jnp.exp(w + o - no2)
                E2 = jnp.exp(kt - no2)
                return ((A2 * p + E2 * vt, A2 * q + E2, no2), y)
            init = (jnp.zeros((Bb, Cc), k.dtype), jnp.zeros((Bb, Cc), k.dtype), jnp.full((Bb, Cc), -1e+38, k.dtype))
            _, yT = jax.lax.scan(step, init, (kT, vT))
            return jnp.swapaxes(yT, 0, 1)
        Tlen = x.shape[1]
        h = _ln(x, g1, b1)
        k = h @ Wk
        v = h @ Wv
        sr = jax.nn.sigmoid(h @ Wr)
        y = _wkv(spatial_decay / Tlen, spatial_first / Tlen, k, v)
        x = x + sr * y @ Wo
        h2 = _ln(x, g2, b2)
        kk = jnp.square(jax.nn.relu(h2 @ Wk_ffn))
        x = x + jax.nn.sigmoid(h2 @ Wr_ffn) * (kk @ Wv_ffn)
        return x

    def _L1_ffn_ref(x, Wr, br, W1, b1, W2, b2):
        import jax, jax.numpy as jnp
        import numpy as np
        D_IN, D_HID, D_OUT = (64, 128, 64)
        N_EXPERTS, TOP_K = (64, 2)
        B, S = (8, 1024)
        Bx, Sx, D = x.shape
        xf = x.reshape(-1, D)
        T = xf.shape[0]
        E = Wr.shape[1]
        logits = xf @ Wr + br
        topk_logits, topk_idx = jax.lax.top_k(logits, TOP_K)
        gates = jax.nn.softmax(topk_logits, axis=1)
        combine = jnp.zeros((T, E), xf.dtype).at[jnp.arange(T)[:, None], topk_idx].add(gates)
        out = jnp.zeros((T, W2.shape[-1]), xf.dtype)
        for e in range(E):
            h = jax.nn.relu(xf @ W1[e] + b1[e])
            y = h @ W2[e] + b2[e]
            out = out + combine[:, e:e + 1] * y
        return out.reshape(Bx, Sx, -1)
    h = _L0_tok_ref(x, L0_tok_W, L0_tok_b)
    h = jnp.concatenate([h, txt], axis=1)
    h = h + _L0_attn_ref(_layernorm(h, axis=-1), L0_attn_ln_w, L0_attn_ln_b, L0_attn_Wu, L0_attn_bu, L0_attn_Wv, L0_attn_bv, L0_attn_Wbase, L0_attn_bbase, L0_attn_q_w, L0_attn_q_b, L0_attn_k_w, L0_attn_k_b, L0_attn_w_rel, L0_attn_Wo, L0_attn_bo)
    h = h + _L0_ffn_ref(_layernorm(h, axis=-1), L0_ffn_hl_w, L0_ffn_hl_b, L0_ffn_wq, L0_ffn_wk, L0_ffn_wv, L0_ffn_gate_w, L0_ffn_gate_b, L0_ffn_ln_g, L0_ffn_ln_b, L0_ffn_fc1_w, L0_ffn_fc1_b, L0_ffn_fc2_w, L0_ffn_fc2_b, L0_ffn_fnorm_g, L0_ffn_fnorm_b, L0_ffn_fgate_w)
    h = h + _L1_attn_ref(_layernorm(h, axis=-1), L1_attn_Wk, L1_attn_Wv, L1_attn_Wr, L1_attn_Wo, L1_attn_Wk_ffn, L1_attn_Wv_ffn, L1_attn_Wr_ffn, L1_attn_g1, L1_attn_b1, L1_attn_g2, L1_attn_b2, L1_attn_spatial_decay, L1_attn_spatial_first)
    h = h + _L1_ffn_ref(_layernorm(h, axis=-1), L1_ffn_Wr, L1_ffn_br, L1_ffn_W1, L1_ffn_b1, L1_ffn_W2, L1_ffn_b2)
    return h

_drawn_inputs = setup_inputs


def setup_inputs(seed=0):
    import zlib

    import numpy as np

    out = dict(_drawn_inputs(seed))
    spreads = {'L0_tok_b': (0.0, 0.1),
     'L0_attn_ln_w': (1.0, 0.2),
     'L0_attn_ln_b': (0.0, 0.372),
     'L0_attn_bu': (0.0, 0.49),
     'L0_attn_bv': (0.0, 0.422),
     'L0_attn_bbase': (0.0, 0.8),
     'L0_attn_q_b': (0.0, 0.8),
     'L0_attn_k_b': (0.0, 0.8),
     'L0_attn_bo': (0.0, 0.1),
     'L0_ffn_ln_g': (1.0, 0.2),
     'L0_ffn_ln_b': (0.0, 0.1),
     'L0_ffn_fnorm_g': (1.0, 0.2),
     'L0_ffn_fnorm_b': (0.0, 0.1)}
    factors = {'L0_attn_Wbase': 8.0,
     'L0_attn_q_w': 8.0,
     'L0_attn_k_w': 8.0,
     'L0_ffn_wq': 6.079,
     'L0_ffn_wk': 7.349,
     'L0_ffn_gate_w': 8.0,
     'L0_ffn_gate_b': 8.0,
     'L0_ffn_fc1_b': 4.079,
     'L1_attn_Wk': 8.0,
     'L1_attn_Wv': 4.452,
     'L1_attn_Wr': 8.0,
     'L1_attn_Wo': 4.599,
     'L1_attn_Wk_ffn': 5.995,
     'L1_attn_Wv_ffn': 6.359,
     'L1_attn_Wr_ffn': 8.0,
     'L1_attn_g1': 8.0,
     'L1_attn_b1': 8.0,
     'L1_attn_g2': 8.0,
     'L1_attn_b2': 8.0,
     'L1_attn_spatial_decay': 8.0,
     'L1_attn_spatial_first': 200.0,
     'L1_ffn_b1': 27.512,
     'L1_ffn_Wr': 8.0,
     'L1_ffn_br': 8.0,
     'L1_ffn_W1': 8.0,
     'L1_ffn_W2': 8.0,
     'L1_ffn_b2': 64.0}
    for name, (base, spread) in spreads.items():
        noise = np.random.default_rng([zlib.crc32(name.encode()), seed]).standard_normal(out[name].shape)
        drawn = base * np.exp(spread * noise) if base else spread * noise
        out[name] = jnp.asarray(drawn.astype(out[name].dtype))
    for name, factor in factors.items():
        out[name] = (out[name] * factor).astype(out[name].dtype)
    return out
```

```python
from contextlib import ExitStack

import numpy as np
import concourse.bass as bass
from concourse import mybir

F32 = mybir.dt.float32
BF16 = mybir.dt.bfloat16
U32 = mybir.dt.uint32
ALU = mybir.AluOpType
ACT = mybir.ActivationFunctionType
AX_X = mybir.AxisListType.X
ds = bass.ds

B, IMG, TXT, D = 128, 224, 32, 64
GRID = 8
NTOK = GRID * GRID + TXT
P = 128
G = 4
NG = B // G
GC = G * D
FC = (G // 2) * NTOK
RB = IMG // 2
NH, NE, DH = 4, 4, 16
NM = NH * NE
NX = 64
SLOT = 128
NBLK = 2 * B * NTOK // SLOT + NX
NHX = 128
EB = 4
CH = B // 4
NU = G * NH
E_ATT = 128
EPS5, EPS8 = 1e-5, 1e-8
B_LINKS, C_LINKS, D_LINKS = 27, 14, 12


def wait(eng, sem, value):
    if isinstance(value, int) and value <= 0:
        return
    eng.wait_ge(sem, value)


def grouped(eng, n, *stages, unroll=2):
    lmax = max(lag for lag, _ in stages)
    lo = -(-(lmax + 2) // unroll) * unroll

    def step(t, first, last):
        for lag, stage in stages:
            if isinstance(t, int) and not first <= t - lag < last:
                continue
            stage(t - lag, (t - lag) % unroll)

    for t in range(lo):
        step(t, 0, n)
    with eng.Fori(lo // unroll, n // unroll) as turn:
        for u in range(unroll):
            for lag, stage in stages:
                stage(turn * unroll + (u - lag), (u - lag) % unroll)
    for t in range(n, n + lmax):
        step(t, 0, n)


class Link:

    def __init__(self, eng, sem, g, per, at=0):
        self.eng, self.sem, self.base, self.per, self.n = eng, sem, g * per + at, per - at, 0

    def __call__(self, ins):
        self.n += 1
        assert self.n <= self.per
        ins.then_inc(self.sem, 1)
        self.eng.wait_ge(self.sem, self.base + self.n)


def build(nc, t_in, out):
    ctx = ExitStack()
    with ctx:
        def sb(name, shape, dt=F32):
            return ctx.enter_context(nc.sbuf_tensor(name, shape, dt))

        def sem(name):
            return ctx.enter_context(nc.semaphore(name))

        class Arena:

            def __init__(self, tile):
                self.tile, self.at = tile, 0

            def __call__(self, name, shape):
                n = int(np.prod(shape[1:]))
                t = self.tile[0:shape[0], self.at:self.at + n]
                self.at += n
                assert self.at <= self.tile.shape[1], name
                dims = " ".join(f"d{i}" for i in range(len(shape) - 1))
                sizes = {f"d{i}": v for i, v in enumerate(shape[1:])}
                return t if len(shape) == 2 else t.rearrange(f"p ({dims}) -> p {dims}", **sizes)

        PS = ctx.enter_context(nc.psum_tensor("PS", [P, 8, 512], F32))
        arena = sb("arena", [P, 22528])
        tabs = Arena(arena)
        tabs.at = 14592

        H = sb("H", [NTOK, B * D])
        XR = sb("XR", [P, B * D])
        ident = sb("ident", [P, P])

        loads, late_loads, zeroed = [], [], []

        def weight(name, shape, *parts):
            w = sb(name, shape)
            for where, src in parts:
                loads.append((w[where], src))
            return w

        def col(v):
            return v.rearrange("(p o) -> p o", o=1)

        lo_, hi_ = slice(0, 64), slice(64, 128)
        every = slice(None)
        loads.append((ident[:, :], t_in["c_ident"]))
        antid = weight("antid", [NTOK, NTOK], ((every, every), t_in["c_antid"]))
        wfilt = weight("wfilt", [RB, 2, 32], ((every, every, every), t_in["c_filt"].rearrange("(c p) f -> p c f", c=2)))
        sel = weight("sel", [7, P], ((every, every), t_in["c_sel"]))
        jmask = weight("jmask", [P, GRID], ((every, every), t_in["c_jmask"]))
        tokw = weight("tokw", [7, D], ((every, every), t_in["L0_tok_W"]))

        def both(name, v):
            return weight(name, [P, 1], ((lo_, every), col(v)), ((hi_, every), col(v)))

        def diagonal(name, w, *more):
            tile = sb(name, [P, 2, w.shape[1]])
            zeroed.append(tile)
            late_loads.extend([(tile[lo_, 0, :], w), (tile[hi_, 1, :], w)])
            return tile

        def swapped_col(name, v):
            return weight(name, [P, 1], ((lo_, every), col(v[64:128])), ((hi_, every), col(v[0:64])))

        tokb = both("tokb", t_in["L0_tok_b"])
        a_lnw = both("a_lnw", t_in["L0_attn_ln_w"])
        a_lnb = both("a_lnb", t_in["L0_attn_ln_b"])
        a_wu = diagonal("a_wu", t_in["L0_attn_Wu"])
        a_wv = diagonal("a_wv", t_in["L0_attn_Wv"])
        a_wb = diagonal("a_wb", t_in["L0_attn_Wbase"])
        wb_dram = t_in["L0_attn_Wbase"]
        a_ws = sb("a_ws", [P, 2, P])
        zeroed.append(a_ws)
        late_loads += [(a_ws[h, k, 64 * c:64 * c + 64], wb_dram[:, 64 - 64 * c:128 - 64 * c])
                       for k, h in enumerate((lo_, hi_)) for c in (0, 1)]
        a_bu = weight("a_bu", [P, 1], ((every, every), col(t_in["L0_attn_bu"])))
        a_bb = weight("a_bb", [P, 1], ((every, every), col(t_in["L0_attn_bbase"])))
        a_bs = swapped_col("a_bs", t_in["L0_attn_bbase"])
        qk_dram = [t_in["L0_attn_" + n].rearrange("o s -> (o s)") for n in ("q_w", "q_b", "k_w", "k_b")]
        a_qk = [weight(f"a_qk{i}", [P, 1], ((every, every), col(v))) for i, v in enumerate(qk_dram)]
        a_qks = [swapped_col(f"a_qks{i}", v) for i, v in enumerate(qk_dram)]
        a_bv = weight("a_bv", [1, G, E_ATT],
                      *[((every, b, every), t_in["L0_attn_bv"].rearrange("(o e) -> o e", o=1)) for b in range(G)])
        a_bo = weight("a_bo", [1, G, D],
                      *[((every, b, every), t_in["L0_attn_bo"].rearrange("(o e) -> o e", o=1)) for b in range(G)])
        a_wo = weight("a_wo", [P, D], ((every, every), t_in["L0_attn_Wo"]))
        ropec = weight("ropec", [P, NTOK], ((every, every), t_in["c_cos"]))
        ropes = weight("ropes", [P, NTOK], ((every, every), t_in["c_sin"]))
        mpe = (t_in["L0_attn_w_rel"].shape[0] + 1) // 2
        rel = t_in["L0_attn_w_rel"]
        hankel = weight("hankel", [NTOK, NTOK], ((every, every),
                        bass.AP(rel.tensor, rel.offset + mpe - NTOK, [[1, NTOK], [1, NTOK]])))

        f_hl = sb("f_hl", [P, 2, D])
        f_wq = sb("f_wq", [P, 2, NE, P])
        f_wk = sb("f_wk", [P, 2, P])
        f_wv = sb("f_wv", [P, 2, D])
        f_gw = sb("f_gw", [P, 2, NH * NE])
        f_fc1 = sb("f_fc1", [P, 1, P])
        f_fc2 = sb("f_fc2", [P, 1, P])
        f_fg = sb("f_fg", [P, 2, NH])
        zeroed += [f_hl, f_wq, f_wk, f_wv, f_gw, f_fc1, f_fc2, f_fg]
        for k in range(2):
            late_loads.append((f_hl[64 * k:64 * k + 64, k, :], t_in["t_hl_w"]))
            late_loads.append((f_fg[64 * k:64 * k + 64, k, :], t_in["t_fgate_w"]))
            for n in range(NH):
                rows = slice(64 * k + DH * n, 64 * k + DH * n + DH)
                late_loads.append((f_wq[rows, k, :, 32 * n:32 * n + DH], t_in["t_wq"][n]))
                late_loads.append((f_wk[rows, k, 32 * n:32 * n + DH], t_in["t_wk"][n]))
                late_loads.append((f_wv[rows, k, DH * n:DH * n + DH], t_in["t_wv"][n]))
                for w, name in ((f_fc1, "fc1_w"), (f_fc2, "fc2_w")):
                    late_loads.append((w[rows, 0, 64 * k + DH * n:64 * k + DH * n + DH],
                                       t_in["t_" + name]))
        for n in range(NH):
            late_loads.append((f_gw[64 * (n % 2):64 * (n % 2) + 64, n // 2, NE * n:NE * n + NE],
                               t_in["t_gate_w"][n]))
        f_hlb = both("f_hlb", t_in["L0_ffn_hl_b"].rearrange("n d -> (n d)"))

        def spread(v, reps, n):
            return bass.AP(v.tensor, v.offset, [[0, reps], [1, n]])
        f_b1 = sb("f_b1", [P, 1])
        f_b2 = sb("f_b2", [P, 1])
        loads += [(w[DH * k:DH * k + DH, :], col(t_in["L0_ffn_" + n]))
                  for w, n in ((f_b1, "fc1_b"), (f_b2, "fc2_b")) for k in range(P // DH)]
        f_gb = weight("f_gb", [1, G, NH * NE],
                      *[((every, b, every), t_in["L0_ffn_gate_b"].rearrange("(o n) e -> o (n e)", o=1)) for b in range(G)])
        f_aff = [weight(f"f_aff{i}", [NTOK, DH], ((every, every), spread(t_in["L0_ffn_" + n], NTOK, DH)))
                 for i, n in enumerate(("ln_g", "ln_b", "fnorm_g", "fnorm_b"))]
        c_wk, c_wv, c_wr, c_wo, c_rf = (diagonal("c_" + n, t_in["L1_attn_" + n]) for n in
                                        ("Wk", "Wv", "Wr", "Wo", "Wr_ffn"))
        c_kf = diagonal("c_kf", t_in["L1_attn_Wk_ffn"])
        HID = t_in["L1_attn_Wk_ffn"].shape[1]
        c_vf = weight("c_vf", [P, 2, D], ((every, every, every), t_in["L1_attn_Wv_ffn"].rearrange("(k p) d -> p k d", k=2)))
        c_g1, c_b1, c_g2, c_b2, c_w, c_u = (both("c_" + n, t_in["L1_attn_" + n]) for n in
                                            ("g1", "b1", "g2", "b2", "spatial_decay", "spatial_first"))
        c_start = tabs("c_start", [P, FC])
        c_decay = tabs("c_decay", [P, FC])
        d_wr = diagonal("d_wr", t_in["L1_ffn_Wr"])
        d_br = weight("d_br", [1, G, NX],
                      *[((every, b, every), t_in["L1_ffn_br"].rearrange("(o e) -> o e", o=1)) for b in range(G)])
        d_tri = weight("d_tri", [NTOK, NTOK], ((every, every), t_in["c_tri"][0:NTOK, 0:NTOK]))
        d_trix = weight("d_trix", [NX, NX], ((every, every), t_in["c_tri"][0:NX, 0:NX]))
        d_iota = weight("d_iota", [NTOK, NBLK], ((every, every), spread(t_in["c_iota"], NTOK, NBLK)))
        d_trib = sb("d_trib", [NTOK, NTOK], BF16)
        d_oneb = sb("d_oneb", [NTOK, 1], BF16)
        onesq = sb("onesq", [P, P])

        cmask = tabs("cmask", [NTOK, NE, NTOK // 2]).bitcast(BF16)
        identb = tabs("identb", [NTOK, NTOK // 2]).bitcast(BF16)

        t0, ta, tb, tc, td = (Arena(arena) for _ in range(5))
        ximg = t0("ximg", [RB, 2, G, 2, IMG])
        Y1 = XR[0:RB, :].rearrange("p (c r n) -> p c r n", c=2, r=4)
        FT = t0("FT", [P, B * GRID])
        wrep = t0("wrep", [P, D])
        gsel = t0("gsel", [P, GRID, D])
        tokF = t0("tokF", [P, (B // 2) * GRID * GRID])

        ones = sb("ones", [1, P])
        mhalf = sb("mhalf", [P, 16])
        stat = sb("stat", [P, 2, 3, 8])
        rstd = sb("rstd", [P, 2, 8])
        xc = sb("xc", [P, 2, GC])
        sq = sb("sq", [P, 2, GC])
        xn = sb("xn", [P, 2, GC])
        xF = sb("xF", [P, 2, FC])

        rq = [tabs(f"rq{i}", [P, NTOK]) for i in range(3)]
        rk = [tabs(f"rk{i}", [P, NTOK]) for i in range(3)]
        rt = tabs("rt", [P, 2, NTOK])
        biasT = tabs("biasT", [NTOK, NTOK])
        Bs = ta("Bs", [P, 2, G * NTOK])
        Bw = ta("Bw", [P, 2, G * NTOK])
        U = ta("U", [P, 2, G * NTOK])
        V = ta("V", [P, 2, G * E_ATT])
        qa = ta("qa", [P, 2, G * NTOK])
        qb = ta("qb", [P, 2, G * NTOK])
        ka = ta("ka", [P, 2, G * NTOK])
        kb = ta("kb", [P, 2, G * NTOK])
        za = ta("za", [P, 2, G * NTOK])
        KT = ta("KT", [P, 2, G * NTOK])
        UO = ta("UO", [P, 2, G * NTOK])

        sxF = tb("sxF", [P, 2, FC])
        qF = tb("qF", [P, 2, NE, G * NTOK])
        kF = tb("kF", [P, 2, G * NTOK])
        Vx = tabs("Vx", [NTOK, 2, G * NH, DH + 1])
        padm = tb("padm", [NTOK, 2, GC])
        resid = tb("resid", [NTOK, D])
        mx = tb("mx", [NTOK, 2, NE])
        Pm = tb("Pm", [NTOK, 2, NE * NTOK])
        Pe = tb("Pe", [NTOK, 2, NE * NTOK])
        PTs = tb("PTs", [NTOK, 2, NE * NTOK])
        oden = tb("oden", [NTOK, NM])
        OT = tb("OT", [NTOK, 2, G, NM * DH])
        OF = tb("OF", [P, 2 * G, NTOK])
        gst = tb("gst", [NTOK, 4, G * NH])
        gd = tb("gd", [NTOK, G * NM])
        ge = tb("ge", [NTOK, G * NM])
        gs = tb("gs", [NTOK, G * NM])
        M1 = tb("M1", [NTOK, G * NM * DH])
        hm = tb("hm", [NTOK, GC])
        hc = tb("hc", [NTOK, GC])
        hs = tb("hs", [NTOK, GC])
        hn = tb("hn", [NTOK, GC])
        hst = tb("hst", [NTOK, 4, G * NH])
        fxF = tb("fxF", [P, FC])
        pmF = tb("pmF", [P, FC])
        h1 = tb("h1", [P, FC])
        yF = tb("yF", [P, FC])
        fo = tb("fo", [NTOK, GC])
        foF = tb("foF", [P, FC])

        xn2 = tc("xn2", [NTOK, 2, GC])
        hst2 = tabs("hst2", [NTOK, 2, 2 * G])
        hc2 = tc("hc2", [NTOK, 2, GC])
        fT2 = tc("fT2", [NTOK, GC])
        X1 = tc("X1", [NTOK, 2, GC])
        X2 = tc("X2", [NTOK, 2, GC])
        kS = tc("kS", [P, 2, FC])
        ukS = tc("ukS", [P, 2, FC])
        vS = tc("vS", [P, 2, FC])
        rS = tc("rS", [P, 2, FC])
        h2F = tc("h2F", [P, FC])
        kr = tc("kr", [P, 2, G * NTOK])
        kk2 = tc("kk2", [P, 2, G * NTOK])
        r2S = tc("r2S", [NTOK, GC])
        Os, Qs, Ns = (tabs(n, [P, FC + 1]) for n in ("Os", "Qs", "Ns"))
        Oq = tc("Oq", [P, FC])
        no = tc("no", [P, FC])
        arg = tc("arg", [P, 4, FC])
        ex = tc("ex", [P, 4, FC])
        w1 = tc("w1", [P, FC])
        w2 = tc("w2", [P, FC])
        w3 = tc("w3", [P, FC])
        w4 = tc("w4", [P, FC])
        sy = tc("sy", [P, FC])
        fT = tc("fT", [NTOK, GC])

        def bf(name, n):
            return td(name, [NTOK, n // 2]).bitcast(BF16)
        OH1, OH2, OHs = (bf(n, B * NX) for n in ("OH1", "OH2", "OHs"))
        OD = td("OD", [NTOK, B * NX])
        Lg = sb("Lg", [NTOK, 2, G, NX])
        m8 = sb("m8", [NTOK, 2, G, 8])
        i8 = sb("i8", [NTOK, 2, G, 8], U32)
        TV = sb("TV", [NTOK, 2, B])
        TI = sb("TI", [NTOK, 2, B])
        TS_ = sb("TS_", [NTOK, 2, B])
        SLu = sb("SLu", [NTOK, 2, B], U32)
        cnt = sb("cnt", [NX, 3, B])
        cs = sb("cs", [NX, 8])
        cmp = sb("cmp", [NX, NBLK])
        blk = sb("blk", [1, NBLK])
        blku = sb("blku", [1, NBLK], U32)
        te = Arena(arena)
        xb = te("xb", [P, 4, EB, D])
        wx = te("wx", [P, 4, EB, NHX + D])
        xT = te("xT", [D + 1, 2, EB * SLOT])
        hT = te("hT", [P, 2, EB * SLOT])
        yb = te("yb", [P, 2, EB, D])
        Y2g = te("Y2g", [NTOK, B * D])
        zt = sb("zt", [P, 1024])
        wpack = t_in["t_experts"]
        XD = nc.dram_tensor("routed_rows", (NBLK * SLOT, D), F32, kind="Internal").ap()
        YD = nc.dram_tensor("expert_rows", (NBLK * SLOT, D), F32, kind="Internal").ap()

        weights_in = sem("weights_in")
        late_in, zeros_set = sem("late_in"), sem("zeros_set")
        txt_in = sem("txt_in")
        img_in = [sem("img_in0"), sem("img_in1")]
        const_set, mask_set = sem("const_set"), sem("mask_set")
        rows_done, rows_kept = sem("rows_done"), sem("rows_kept")
        cols_done, cols_kept = sem("cols_done"), sem("cols_kept")
        wrep_done, gsel_done = sem("wrep_done"), sem("gsel_done")
        tok_done, tok_kept = sem("tok_done"), sem("tok_kept")
        tokT_done, tokT_kept = sem("tokT_done"), sem("tokT_kept")
        hank_done, rope_chain, rope_set = sem("hank_done"), sem("rope_chain"), sem("rope_set")
        ln_chain = sem("ln_chain")
        ln_var, ln_rstd, ln_xn = sem("ln_var"), sem("ln_rstd"), sem("ln_xn")
        ln_xT, ln_xF = sem("ln_xT"), sem("ln_xF")
        a_proj, a_silu = sem("a_proj"), sem("a_silu")
        a_rope, a_kpart, a_ropec = sem("a_rope"), sem("a_kpart"), sem("a_ropec")
        a_qk_done, a_kern, a_kernc = sem("a_qk_done"), sem("a_kern"), sem("a_kernc")
        a_av, a_uo, a_wo_done, a_h = sem("a_av"), sem("a_uo"), sem("a_wo_done"), sem("a_h")
        (b_sx, b_sxF, b_vs, b_vx, b_pad, b_k, b_kk, b_q, b_qk, b_s, b_max, b_sub, b_exp, b_pt, b_ptk, b_av, b_oc, b_o, b_om, b_oT, b_oF, b_gate, b_gd, b_ge, b_chain, b_gs, b_m1, b_pw1, b_r1, b_hn, b_fxT, b_fxF, b_fc1, b_h1, b_fc2, b_y, b_yT, b_pw2, b_r2, b_fo, b_foT, b_foF, b_fg, b_wd, b_we, b_h) = map(sem, (
            "b_sx b_sxF b_vs b_vx b_pad b_k b_kk b_q b_qk b_s b_max b_sub b_exp b_pt b_ptk b_av b_oc b_o b_om b_oT b_oF b_gate b_gd b_ge b_chain b_gs b_m1 b_pw1 b_r1 b_hn b_fxT b_fxF b_fc1 b_h1 b_fc2 b_y b_yT b_pw2 b_r2 b_fo b_foT b_foF b_fg b_wd b_we b_h").split())
        (c_kv, c_kvS, c_chain, c_arg, c_exp, c_sy, c_wod, c_x1, c_x2, c_var2, c_rstd2, c_xn2, c_xT2, c_h2F, c_ff, c_krS, c_kkS, c_r2S, c_vfd, c_fc, c_h, tab_set) = map(sem, (
            "c_kv c_kvS c_chain c_arg c_exp c_sy c_wod c_x1 c_x2 c_var2 c_rstd2 c_xn2 c_xT2 c_h2F c_ff c_krS c_kkS c_r2S c_vfd c_fc c_h tab_set").split())
        c_tab = sem("c_tab")
        out_sem = sem("out_sem")
        (d_xr, d_lg, d_lgS, d_m8, d_i8, d_top, d_chain, d_diff, d_exp, d_oh, d_cnt, d_nblk, d_base, d_off, d_rank, d_rankS, d_slots, d_cmp, d_blkp, d_blk, zeros_out, scat, e_ones, e_xT, e_xTs, e_up, e_h, e_down, e_y, e_go, d_go, d_sum, d_comb) = map(sem, (
            "d_xr d_lg d_lgS d_m8 d_i8 d_top d_chain d_diff d_exp d_oh d_cnt d_nblk d_base d_off d_rank d_rankS d_slots d_cmp d_blkp d_blk zeros_out scat e_ones e_xT e_xTs e_up e_h e_down e_y e_go d_go d_sum d_comb").split())
        e_in = [sem(f"e_in{u}") for u in range(4)]
        e_st = [sem(f"e_st{u}") for u in range(2)]
        gath = [sem(f"gath{c}") for c in range(4)]

        block = ctx.enter_context(nc.Block())
        x_img = t_in["x"].rearrange("(g i) o (c p) w -> g p (i o c) w", i=G, c=2)

        def bank(i, parts, cols):
            return PS[0:parts, i, 0:cols]

        def hgroup(g):
            return H[:, ds(g * GC, GC)]

        def ln_sums(eng, g, u, k):
            c = ln_chain
            c0 = k * NG * 5 + g * 5
            v = hgroup(g).rearrange("p (b d) -> p b d", d=D)
            s = stat[0:NTOK, u, 0, 0:G]
            m = stat[0:NTOK, u, 1, 0:G]
            xcg, sqg = xc[0:NTOK, u, :], sq[0:NTOK, u, :]
            eng.tensor_reduce(s, v, AX_X, ALU.add).then_inc(c, 1)
            eng.wait_ge(c, c0 + 1)
            eng.tensor_scalar(m, s, -1.0 / D, None, ALU.mult).then_inc(c, 1)
            eng.wait_ge(c, c0 + 2)
            eng.tensor_tensor(xcg.rearrange("p (b d) -> p b d", d=D), v,
                              m.unsqueeze(2).broadcast_to([NTOK, G, D]), ALU.add).then_inc(c, 1)
            eng.wait_ge(c, c0 + 3)
            eng.tensor_tensor(sqg, xcg, xcg, ALU.mult).then_inc(c, 1)
            eng.wait_ge(c, c0 + 4)
            eng.tensor_reduce(s, sqg.rearrange("p (b d) -> p b d", d=D), AX_X, ALU.add).then_inc(c, 1)
            eng.wait_ge(c, c0 + 5)

        @block.sync
        def _(sp):
            for dst, src in loads:
                sp.dma_start(dst, src).then_inc(weights_in, 16)
            sp.wait_ge(zeros_set, len(zeroed) + 1)
            for dst, src in late_loads:
                sp.dma_start(dst, src).then_inc(late_in, 16)
            sp.dma_start(H[GRID * GRID:NTOK, :].rearrange("p (b d) -> p b d", d=D),
                         t_in["txt"].rearrange("b t d -> t b d")).then_inc(txt_in, 16)

            def load_images(g, u):
                wait(sp, rows_done, g - 1)
                sp.dma_start(ximg[:, u, :, :, :].rearrange("p i c w -> p (i c) w"),
                             x_img[ds(g, 1)].rearrange("o p n w -> p (o n) w")).then_inc(img_in[u], 16)
            grouped(sp, NG, (0, load_images))
            sp.wait_ge(zeros_set, len(zeroed) + 1)
            xd = XD.rearrange("(n p r) d -> n p (r d)", p=P, r=1024 // D)
            for n in range(xd.shape[0]):
                sp.dma_start(xd[n], zt[:, :]).then_inc(zeros_out, 16)

            def load_blocks(g, u):
                wait(sp, e_down, g - 3)
                sp.dma_start(xb[:, u, :, :], XD[ds(g * (EB * SLOT), EB * SLOT)].rearrange("(k p) d -> p k d", p=P)
                             ).then_inc(e_in[u], 16)
                for k in range(EB):
                    e = sp.value_load(blku[0:1, ds(g * EB + k, 1)], min_val=0, max_val=NX - 1)
                    sp.dma_start(wx[:, u, k, :], wpack[ds(e, 1)].rearrange("o p w -> p (o w)")).then_inc(e_in[u], 16)

            def store_blocks(g, u):
                sp.wait_ge(e_y, g + 1)
                sp.dma_start(YD[ds(g * (EB * SLOT), EB * SLOT)].rearrange("(k p) d -> p k d", p=P),
                             yb[:, u % 2, :, :]).then_inc(e_st[u % 2], 16)

            sp.wait_ge(scat, 16 * 2 * B)
            sp.wait_ge(d_blk, 1)
            grouped(sp, NBLK // EB, (0, load_blocks), (3, store_blocks), unroll=4)
            for c in range(B // CH):
                sp.wait_ge(d_comb, c + 1)
                sp.dma_start(out[c * CH:(c + 1) * CH].rearrange("b t d -> t b d"),
                             H[:, c * CH * D:(c + 1) * CH * D].rearrange("p (b d) -> p b d", d=D)).then_inc(out_sem, 16)
            sp.wait_ge(out_sem, 16 * (B // CH))

        @block.tensor
        def _(pe):
            pe.wait_ge(weights_in, 16 * len(loads))
            pe.wait_ge(const_set, 7)

            def image_rows(g, u):
                wait(pe, rows_kept, g - 1)
                half = (g - u) // 2 if isinstance(g, int) else None
                pe.wait_ge(img_in[u], (g - u) * 8 + 16)
                for i in range(G):
                    for c in range(2):
                        for r in range(2):
                            mm = pe.matmul(PS[0:RB, u, (c * G + i) * 32:(c * G + i + 1) * 32],
                                           ximg[:, u, i, r, c * RB:(c + 1) * RB], wfilt[:, r, :],
                                           start=(r == 0), stop=(r == 1))
                mm.then_inc(rows_done, 1)
            grouped(pe, NG, (0, image_rows))

            pe.wait_ge(rows_kept, NG)
            for h in range(2):
                for r in range(4):
                    for c in range(2):
                        mm = pe.matmul(PS[32 * r:32 * r + 32, 2 + h, :], wfilt[:, c, :],
                                       Y1[:, c, r, 512 * h:512 * h + 512], start=(c == 0), stop=(c == 1))
                mm.then_inc(cols_done, 1)
            pe.matmul(bank(4, P, D), sel[:, :], tokw[:, :], start=True, stop=True).then_inc(wrep_done, 1)
            pe.transpose(bank(5, NTOK, NTOK), hankel[:, :], antid[:, :]).then_inc(hank_done, 1)
            pe.wait_ge(cols_kept, 2)
            pe.wait_ge(gsel_done, GRID)
            fv = FT[:, :].rearrange("p (b q i) -> p q b i", q=2, i=GRID)
            for j in range(GRID):
                wait(pe, tok_kept, j - 1)
                for par in range(2):
                    mm = pe.matmul(PS[64 * par:64 * par + 64, 6 + j % 2, :], gsel[:, j, :], fv[:, par],
                                   start=True, stop=True)
                mm.then_inc(tok_done, 1)
            pe.wait_ge(tok_kept, GRID)
            for k in range(B // 8):
                wait(pe, tokT_kept, k - 1)
                for q in range(4):
                    p = 4 * k + q
                    mm = pe.transpose(PS[0:64, k % 2, q * P:(q + 1) * P], tokF[:, p * 64:(p + 1) * 64],
                                      ident[:, :])
                mm.then_inc(tokT_done, 1)

            T_, B_, S_, U_, V_, K_, O_, W_ = range(8)
            pe.wait_ge(tokT_kept, B // 8)
            pe.wait_ge(rope_set, 1)
            pe.wait_ge(late_in, 16 * len(late_loads))

            def a_transpose(g, u):
                wait(pe, ln_xF, g)
                pe.wait_ge(ln_xn, g + 1)
                for q in range(2):
                    mm = pe.transpose(PS[:, T_, q * NTOK:(q + 1) * NTOK], xn[0:NTOK, u, q * P:(q + 1) * P],
                                      ident[0:NTOK, 0:NTOK])
                mm.then_inc(ln_xT, 1)

            def a_project(g, u):
                pe.wait_ge(ln_xF, g + 1)
                wait(pe, a_silu, g * 4)
                for bk, w in ((B_, a_wb), (S_, a_ws), (U_, a_wu)):
                    for par in range(2):
                        o = PS[:, bk, 0:G * NTOK].rearrange("p (q r t) -> p q r t", q=2, r=2)[:, :, par, :]
                        mm = pe.matmul(o, w[:, par, :], xF[:, u, :].rearrange("p (q t) -> p q t", q=2),
                                       start=True, stop=True)
                    mm.then_inc(a_proj, 1)
                pe.matmul(PS[0:NTOK, V_, :], ones[:, 0:NTOK], a_bv[:, :, :].rearrange("p b e -> p (b e)"),
                          start=True, stop=True)
                for q in range(2):
                    mm = pe.matmul(PS[0:NTOK, V_, q * 256:(q + 1) * 256], xF[:, u, q * NTOK:(q + 1) * NTOK],
                                   a_wv[:, :, :].rearrange("p k e -> p (k e)"), start=False, stop=True,
                                   skip_group_check=True)
                mm.then_inc(a_proj, 1)

            def a_scores(g, u):
                pe.wait_ge(a_rope, g + 1)
                wait(pe, a_kern, g)
                for b in range(G):
                    t = slice(b * NTOK, (b + 1) * NTOK)
                    mm = pe.matmul(PS[0:NTOK, K_, t], ka[:, u, t], qa[:, u, t], start=True, stop=True)
                mm.then_inc(a_qk_done, 1)

            def a_attend(g, u):
                pe.wait_ge(a_kern, g + 1)
                pe.wait_ge(a_silu, g * 4 + 4)
                wait(pe, a_uo, g)
                for b in range(G):
                    t = slice(b * NTOK, (b + 1) * NTOK)
                    mm = pe.matmul(PS[:, O_, t], V[0:NTOK, u, b * E_ATT:(b + 1) * E_ATT], KT[0:NTOK, u, t],
                                   start=True, stop=True)
                mm.then_inc(a_av, 1)

            def a_output(g, u):
                pe.wait_ge(a_uo, g + 1)
                wait(pe, a_h, g)
                pe.matmul(bank(W_, NTOK, GC), ones[:, 0:NTOK], a_bo[:, :, :].rearrange("p b e -> p (b e)"),
                          start=True, stop=True)
                for b in range(G):
                    mm = pe.matmul(PS[0:NTOK, W_, b * D:(b + 1) * D], UO[:, u, b * NTOK:(b + 1) * NTOK],
                                   a_wo[:, :], start=False, stop=True, skip_group_check=True)
                mm.then_inc(a_wo_done, 1)

            grouped(pe, NG, (1, a_transpose), (1, a_project), (2, a_scores), (2, a_attend), (2, a_output))

            pe.wait_ge(a_h, NG)
            pe.wait_ge(mask_set, 2)
            O_, F_, Q_, Z_ = 4, 5, 6, 7

            def to_features(src, dst_bank, rows=NTOK):
                for q in range(2):
                    mm = pe.transpose(PS[:, dst_bank, q * NTOK:(q + 1) * NTOK], src[:, q * P:(q + 1) * P],
                                      ident[0:NTOK, 0:NTOK])
                return mm

            def to_tokens(src, dst_bank, at=0):
                for q in range(2):
                    mm = pe.transpose(PS[0:NTOK, dst_bank, at + q * P:at + (q + 1) * P],
                                      src[:, q * NTOK:(q + 1) * NTOK], ident[:, :])
                return mm

            def b_transpose(g, u):
                pe.wait_ge(ln_xn, NG + g + 1)
                wait(pe, b_vx, g)
                wait(pe, b_pad, g)
                to_features(xn[0:NTOK, u, :], F_).then_inc(ln_xT, 1)

            def b_heads(g, u):
                pe.wait_ge(ln_xF, NG + g + 1)
                pe.matmul(bank(F_, P, FC), f_hl[:, :, :].rearrange("p k d -> p (k d)"), xF[:, u, :],
                          start=True, stop=True).then_inc(b_sx, 1)

            def b_values(g, u):
                pe.wait_ge(b_sxF, g + 1)
                for q in range(2):
                    pe.matmul(PS[0:NTOK, F_, q * P:(q + 1) * P], sxF[:, u, q * NTOK:(q + 1) * NTOK],
                              f_wv[:, :, :].rearrange("p k d -> p (k d)"), start=True, stop=True)
                to_tokens(sxF[:, u, :], F_, GC).then_inc(b_vs, 1)

            def project(w, u, bk):
                for par in range(2):
                    o = PS[:, bk, 0:G * NTOK].rearrange("p (q r t) -> p q r t", q=2, r=2)[:, :, par, :]
                    mm = pe.matmul(o, w[:, par, :], sxF[:, u, :].rearrange("p (q t) -> p q t", q=2),
                                   start=True, stop=True)
                return mm

            def b_keys(g, u):
                wait(pe, b_qk, g * NE)
                wait(pe, b_oF, g * 2 - 2)
                project(f_wk, u, Q_).then_inc(b_k, 1)

            def b_query(e):
                def stage(g, u):
                    pe.wait_ge(b_kk, g + 1)
                    wait(pe, b_qk, g * NE + e)
                    project(f_wq[:, :, e, :], u, Q_).then_inc(b_q, 1)
                return stage

            def b_slots(k0, k1):
                def stage(g, u):
                    for k in range(k0, k1):
                        if k < NU:
                            b, n, n0 = k // NH, k % NH, 32 * (k % NH)
                            if k == 0:
                                pe.wait_ge(b_qk, (g + 1) * NE)
                            wait(pe, b_sub, g * NU + (k - 1))
                            pe.matmul(bank(k % 2, NTOK, NE * NTOK), identb[:, :],
                                      cmask[:, :, :].rearrange("p e t -> p (e t)"), start=True, stop=True)
                            for e in range(NE):
                                mm = pe.matmul(PS[0:NTOK, k % 2, e * NTOK:(e + 1) * NTOK],
                                               qF[n0:n0 + DH, u, e, b * NTOK:(b + 1) * NTOK],
                                               kF[n0:n0 + DH, u, b * NTOK:(b + 1) * NTOK],
                                               start=False, stop=True, skip_group_check=True)
                            mm.then_inc(b_s, 1)
                        if 0 <= k - 1 < NU:
                            j = k - 1
                            pe.wait_ge(b_exp, g * NU + (j + 1))
                            wait(pe, b_ptk, g * NU + (j - 1))
                            for e in range(NE):
                                t = slice(e * NTOK, (e + 1) * NTOK)
                                mm = pe.transpose(PS[0:NTOK, 2 + j % 2, t], Pe[:, j % 2, t], ident[0:NTOK, 0:NTOK])
                            mm.then_inc(b_pt, 1)
                        if 0 <= k - 2 < NU:
                            j = k - 2
                            b, n = j // NH, j % NH
                            pe.wait_ge(b_ptk, g * NU + (j + 1))
                            if n == 0:
                                wait(pe, b_o, g * G + b)
                            if j == 0:
                                pe.wait_ge(b_vx, g + 1)
                            for e in range(NE):
                                c = (n * NE + e) * (DH + 1)
                                mm = pe.matmul(PS[0:NTOK, O_, c:c + DH + 1], PTs[:, j % 2, e * NTOK:(e + 1) * NTOK],
                                               Vx[:, u, b * NH + n, :], start=True, stop=True)
                            mm.then_inc(b_av, 1)
                return stage

            def b_outT(g, u):
                pe.wait_ge(b_om, (g + 1) * G)
                wait(pe, b_wd, g)
                for b in range(G):
                    if b == 2:
                        pe.wait_ge(b_qk, (min(g + 2, NG) if isinstance(g, int) else g + 2) * NE)
                    for h in range(2):
                        c = (b % 2) * 2 + h
                        mm = pe.transpose(PS[:, (Z_, Q_)[b // 2], c * NTOK:(c + 1) * NTOK],
                                          OT[:, u, b, h * P:(h + 1) * P], ident[0:NTOK, 0:NTOK])
                    if b % 2:
                        mm.then_inc(b_oT, 1)

            def b_gates(g, u):
                pe.wait_ge(b_oF, g * 2 + 2)
                pe.matmul(bank(Z_, NTOK, G * NM), ones[:, 0:NTOK], f_gb[:, :, :].rearrange("p b e -> p (b e)"),
                          start=True, stop=True)
                for b in range(G):
                    for h in range(2):
                        mm = pe.matmul(PS[0:NTOK, Z_, b * NM:(b + 1) * NM], OF[:, b * 2 + h, :], f_gw[:, h, :],
                                       start=False, stop=True, skip_group_check=True)
                mm.then_inc(b_gate, 1)

            def b_fx(g, u):
                pe.wait_ge(b_hn, g + 1)
                to_features(hn[:, :], Z_).then_inc(b_fxT, 1)

            def b_fc1s(g, u):
                pe.wait_ge(b_fxF, g + 1)
                pe.matmul(bank(Z_, P, FC), f_fc1[:, 0, :], fxF[:, :], start=True, stop=True).then_inc(b_fc1, 1)

            def b_fc2s(g, u):
                pe.wait_ge(b_h1, g + 1)
                pe.matmul(bank(Z_, P, FC), f_fc2[:, 0, :], h1[:, :], start=True, stop=True).then_inc(b_fc2, 1)

            def b_yTs(g, u):
                pe.wait_ge(b_y, g + 1)
                to_tokens(yF[:, :], Z_).then_inc(b_yT, 1)

            def b_foTs(g, u):
                pe.wait_ge(b_fo, g + 1)
                to_features(fo[:, :], Z_).then_inc(b_foT, 1)

            def b_fgates(g, u):
                pe.wait_ge(b_foF, g + 1)
                for q in range(2):
                    mm = pe.matmul(PS[0:NTOK, Z_, q * 2 * NH:(q + 1) * 2 * NH], foF[:, q * NTOK:(q + 1) * NTOK],
                                   f_fg[:, :, :].rearrange("p k n -> p (k n)"), start=True, stop=True)
                mm.then_inc(b_fg, 1)

            grouped(pe, NG, (3, b_outT), (2, b_slots(0, 2)), (3, b_gates), (1, b_transpose), (2, b_slots(2, 3)),
                    (1, b_heads), (2, b_slots(3, 4)), (1, b_values), (2, b_slots(4, 5)), (1, b_keys),
                    (2, b_slots(5, 6)), (1, b_query(0)), (2, b_slots(6, 7)), (1, b_query(1)), (3, b_fx),
                    (2, b_slots(7, 8)), (1, b_query(2)), (3, b_fc1s), (2, b_slots(8, 9)), (1, b_query(3)),
                    (3, b_fc2s), (2, b_slots(9, 11)), (3, b_yTs), (2, b_slots(11, 14)), (3, b_foTs),
                    (2, b_slots(14, 15)), (3, b_fgates), (2, b_slots(15, 18)))

            pe.wait_ge(b_h, NG)
            T_, A_, R_, OO, T2, K0, K1, ZZ = range(8)

            def c_transpose(g, u):
                pe.wait_ge(ln_xn, 2 * NG + g + 1)
                wait(pe, ln_xF, 2 * NG + g)
                to_features(xn[0:NTOK, u, :], T_).then_inc(ln_xT, 1)

            def flat(w):
                return w[:, :, :].rearrange("p k d -> p (k d)")

            def c_kvr(g, u):
                pe.wait_ge(ln_xF, 2 * NG + g + 1)
                wait(pe, c_kvS, g)
                pe.matmul(PS[:, A_, 0:FC], flat(c_wk), xF[:, u, :], start=True, stop=True)
                pe.matmul(PS[:, A_, FC:2 * FC], flat(c_wv), xF[:, u, :], start=True, stop=True)
                pe.matmul(PS[:, R_, 0:FC], flat(c_wr), xF[:, u, :], start=True, stop=True).then_inc(c_kv, 1)

            def c_out(g, u):
                pe.wait_ge(c_sy, g + 1)
                wait(pe, c_x2, g)
                for q in range(2):
                    mm = pe.matmul(PS[0:NTOK, OO, q * P:(q + 1) * P], sy[:, q * NTOK:(q + 1) * NTOK], flat(c_wo),
                                   start=True, stop=True)
                mm.then_inc(c_wod, 1)

            def c_transpose2(g, u):
                pe.wait_ge(c_xn2, g + 1)
                wait(pe, c_h2F, g)
                to_features(xn2[:, u, :], T2).then_inc(c_xT2, 1)

            def c_mix(g, u):
                pe.wait_ge(c_h2F, g + 1)
                wait(pe, c_krS, g)
                wait(pe, c_h, g)
                for h, bk in enumerate((K0, K1)):
                    for par in range(2):
                        o = PS[:, bk, 0:G * NTOK].rearrange("p (q r t) -> p q r t", q=2, r=2)[:, :, par, :]
                        mm = pe.matmul(o, c_kf[:, par, h * P:(h + 1) * P], h2F[:, :].rearrange("p (q t) -> p q t", q=2),
                                       start=True, stop=True)
                for q in range(2):
                    mm = pe.matmul(PS[0:NTOK, ZZ, q * P:(q + 1) * P], h2F[:, q * NTOK:(q + 1) * NTOK], flat(c_rf),
                                   start=True, stop=True)
                mm.then_inc(c_ff, 1)

            def c_values(g, u):
                pe.wait_ge(c_kkS, g + 1)
                pe.wait_ge(c_r2S, g + 1)
                for b in range(G):
                    for h in range(2):
                        mm = pe.matmul(PS[0:NTOK, ZZ, GC + b * D:GC + (b + 1) * D], kk2[:, h, b * NTOK:(b + 1) * NTOK],
                                       c_vf[:, h, :], start=(h == 0), stop=(h == 1))
                mm.then_inc(c_vfd, 1)

            grouped(pe, NG, (1, c_transpose), (3, c_transpose2), (1, c_kvr), (3, c_mix), (2, c_out), (3, c_values))

            pe.wait_ge(c_h, NG)

            def d_transpose(g, u):
                pe.wait_ge(ln_xn, 3 * NG + g + 1)
                wait(pe, ln_xF, 3 * NG + g)
                to_features(xn[0:NTOK, u, :], 0).then_inc(ln_xT, 1)

            def d_logits(g, u):
                pe.wait_ge(ln_xF, 3 * NG + g + 1)
                wait(pe, d_lgS, g)
                pe.matmul(bank(1, NTOK, G * NX), ones[:, 0:NTOK], d_br[:, :, :].rearrange("p b e -> p (b e)"),
                          start=True, stop=True)
                for q in range(2):
                    mm = pe.matmul(PS[0:NTOK, 1, q * 2 * NX:(q + 1) * 2 * NX], xF[:, u, q * NTOK:(q + 1) * NTOK],
                                   flat(d_wr), start=False, stop=True, skip_group_check=True)
                mm.then_inc(d_lg, 1)

            grouped(pe, NG, (1, d_transpose), (1, d_logits))

            pe.wait_ge(d_oh, 3)
            for b in range(B):
                mm = pe.matmul(PS[0:NX, 2, b:b + 1], OHs[:, b * NX:(b + 1) * NX], d_oneb[:, :], start=True, stop=True)
            mm.then_inc(d_cnt, 1)
            pe.wait_ge(d_nblk, 1)
            pe.matmul(PS[0:NX, 3, 0:1], d_trix[:, :], cs[:, 0:1], start=True, stop=True).then_inc(d_base, 1)
            pe.wait_ge(d_cmp, 1)
            pe.matmul(PS[0:1, 3, 0:NBLK], onesq[0:NX, 0:1], cmp[:, :], start=True, stop=True).then_inc(d_blkp, 1)
            pe.wait_ge(d_off, 1)

            def d_ranks(g, u):
                wait(pe, d_rankS, g - 1)
                pe.matmul(bank(4 + u, NTOK, 512), onesq[0:NX, 0:NTOK], OD[0:NX, ds(g * 512, 512)], start=True, stop=False)
                pe.matmul(bank(4 + u, NTOK, 512), d_trib[:, :], OHs[:, ds(g * 512, 512)], start=False,
                          stop=True).then_inc(d_rank, 1)
            grouped(pe, B // 8, (0, d_ranks))

            pe.wait_ge(e_ones, 2)

            def e_transpose(g, u):
                pe.wait_ge(e_in[u], (g - u) * (4 * (1 + EB)) + 16 * (1 + EB))
                wait(pe, e_xTs, g - 1)
                pe.sem_inc(e_go, 1)
                for k in range(EB):
                    mm = pe.transpose(PS[0:D, u % 2, k * SLOT:(k + 1) * SLOT], xb[:, u, k, :], ident[:, :])
                mm.then_inc(e_xT, 1)

            def e_hidden(g, u):
                pe.wait_ge(e_xTs, g + 1)
                wait(pe, e_h, g - 1)
                for k in range(EB):
                    mm = pe.matmul(PS[:, 2 + u % 2, k * SLOT:(k + 1) * SLOT], wx[0:D + 1, u, k, 0:NHX],
                                   xT[:, u % 2, k * SLOT:(k + 1) * SLOT], start=True, stop=True)
                mm.then_inc(e_up, 1)

            def e_output(g, u):
                pe.wait_ge(e_h, g + 1)
                wait(pe, e_y, g - 1)
                for k in range(EB):
                    o = PS[:, 4 + u % 2, k * D:(k + 1) * D]
                    pe.matmul(o, hT[:, u % 2, k * SLOT:(k + 1) * SLOT], wx[:, u, k, NHX:NHX + D], start=True, stop=False)
                    mm = pe.matmul(o, onesq[96:97, :], wx[96:97, u, k, 0:D], start=False, stop=True)
                mm.then_inc(e_down, 1)

            grouped(pe, NBLK // EB, (0, e_transpose), (2, e_output), (1, e_hidden), unroll=4)

        @block.scalar
        def _(act):
            act.wait_ge(weights_in, 16 * len(loads))

            def keep_rows(g, u):
                act.wait_ge(rows_done, g + 1)
                for c in range(2):
                    o = Y1[:, c, :, ds(g * (G * GRID), G * GRID)].rearrange("p r (n i) -> p r n i", i=GRID)
                    i_ = PS[0:RB, u, c * G * 32:(c + 1) * G * 32].rearrange("p (n r i) -> p r n i", n=G, r=4)
                    a = act.activation(o, i_, ACT.Identity)
                a.then_inc(rows_kept, 1)
            grouped(act, NG, (0, keep_rows))
            for h in range(2):
                act.wait_ge(cols_done, h + 1)
                act.activation(FT[:, 512 * h:512 * h + 512], bank(2 + h, P, 512), ACT.Identity).then_inc(cols_kept, 1)
            for j in range(GRID):
                act.wait_ge(tok_done, j + 1)
                o = tokF[:, :].rearrange("p (b i j) -> p b i j", i=GRID, j=GRID)[:, :, :, j]
                act.activation(o, PS[:, 6 + j % 2, :].rearrange("p (b i) -> p b i", i=GRID), ACT.Identity,
                               bias=tokb[:, :]).then_inc(tok_kept, 1)
            for k in range(B // 8):
                act.wait_ge(tokT_done, k + 1)
                act.activation(H[0:64, k * 512:(k + 1) * 512], bank(k % 2, 64, 512), ACT.Identity).then_inc(tokT_kept, 1)

            T_, B_, S_, U_, V_ = range(5)

            def a_features(g, u):
                act.wait_ge(ln_xT, g + 1)
                wait(act, a_proj, (g - 1) * 4)
                act.activation(xF[:, u, :], bank(T_, P, FC), ACT.Identity, bias=a_lnb[:, :],
                               scale=a_lnw[:, :]).then_inc(ln_xF, 1)

            def a_silus(g, u):
                wait(act, a_rope, g - 1)
                wait(act, a_uo, g - 1)
                for k, (bk, dst, bias) in enumerate(((B_, Bs, a_bb), (S_, Bw, a_bs), (U_, U, a_bu))):
                    act.wait_ge(a_proj, g * 4 + k + 1)
                    act.activation(dst[:, u, :], bank(bk, P, G * NTOK), ACT.Silu, bias=bias[:, :]).then_inc(a_silu, 1)
                act.wait_ge(a_proj, g * 4 + 4)
                act.activation(V[0:NTOK, u, :], bank(V_, NTOK, 512), ACT.Silu).then_inc(a_silu, 1)

            grouped(act, NG, (1, a_features), (1, a_silus))

            act.wait_ge(a_h, NG)
            O_, F_, Q_, Z_ = 4, 5, 6, 7

            def copy_out(dst, src, **kw):
                return act.activation(dst, src, ACT.Identity, **kw)

            def b_features(g, u):
                act.wait_ge(ln_xT, NG + g + 1)
                copy_out(xF[:, u, :], bank(F_, P, FC)).then_inc(ln_xF, 1)

            def b_headF(g, u):
                act.wait_ge(b_sx, g + 1)
                copy_out(sxF[:, u, :], bank(F_, P, FC), bias=f_hlb[:, :]).then_inc(b_sxF, 1)

            def b_valuesV(g, u):
                act.wait_ge(b_vs, g + 1)
                act.wait_ge(b_pad, g + 1)
                wait(act, b_av, (g - 1) * NU)
                copy_out(Vx[:, u, :, 0:DH], bank(F_, NTOK, GC).rearrange("p (n d) -> p n d", d=DH)).then_inc(b_vx, 1)

            def b_keysK(g, u):
                act.wait_ge(b_k, g + 1)
                wait(act, b_s, (g - 1) * NU)
                act.activation(kF[:, u, :], bank(Q_, P, G * NTOK), ACT.Identity,
                               scale=float(DH) ** 0.5).then_inc(b_kk, 1)

            def b_queryQ(e):
                def stage(g, u):
                    act.wait_ge(b_q, g * NE + (e + 1))
                    copy_out(qF[:, u, e, :], bank(Q_, P, G * NTOK)).then_inc(b_qk, 1)
                return stage

            def b_slots(k0, k1):
                def stage(g, u):
                    for k in range(k0, k1):
                        if k < NU:
                            act.wait_ge(b_sub, g * NU + (k + 1))
                            wait(act, b_pt, g * NU + (k - 1))
                            act.activation(Pe[:, k % 2, :], Pm[:, k % 2, :], ACT.Exp).then_inc(b_exp, 1)
                        if 0 <= k - 1 < NU:
                            j = k - 1
                            act.wait_ge(b_pt, g * NU + (j + 1))
                            wait(act, b_av, g * NU + (j - 1))
                            copy_out(PTs[:, j % 2, :], bank(2 + j % 2, NTOK, NE * NTOK)).then_inc(b_ptk, 1)
                return stage

            def b_outF(g, u):
                wait(act, b_gate, g)
                for h in range(2):
                    act.wait_ge(b_oT, g * 2 + h + 1)
                    copy_out(OF[:, 4 * h:4 * h + 4, :], bank((Z_, Q_)[h], P, 4 * NTOK)
                             .rearrange("p (c t) -> p c t", c=4)).then_inc(b_oF, 1)

            def b_gexp(g, u):
                act.wait_ge(b_gd, g + 1)
                act.activation(ge[:, :], gd[:, :], ACT.Exp).then_inc(b_ge, 1)

            def b_fxFs(g, u):
                act.wait_ge(b_fxT, g + 1)
                wait(act, b_y, g)
                copy_out(fxF[:, :], bank(Z_, P, FC)).then_inc(b_fxF, 1)

            def b_foFs(g, u):
                act.wait_ge(b_foT, g + 1)
                wait(act, b_fg, g)
                copy_out(foF[:, :], bank(Z_, P, FC)).then_inc(b_foF, 1)

            def b_wexp(g, u):
                act.wait_ge(b_wd, g + 1)
                act.activation(ge[:, 0:G * NH], gd[:, 0:G * NH], ACT.Exp).then_inc(b_we, 1)

            grouped(act, NG, (3, b_outF), (2, b_slots(0, 2)), (1, b_features), (2, b_slots(2, 3)),
                    (3, b_gexp), (1, b_headF), (2, b_slots(3, 4)), (1, b_valuesV), (2, b_slots(4, 5)), (1, b_keysK),
                    (2, b_slots(5, 6)), (1, b_queryQ(0)), (2, b_slots(6, 7)), (1, b_queryQ(1)), (3, b_fxFs),
                    (2, b_slots(7, 8)), (1, b_queryQ(2)), (2, b_slots(8, 9)), (1, b_queryQ(3)),
                    (2, b_slots(9, 14)), (3, b_foFs), (2, b_slots(14, 16)), (3, b_wexp), (2, b_slots(16, 17)))

            act.wait_ge(b_h, NG)
            act.wait_ge(tab_set, 3)
            T_, A_, R_, OO, T2, K0, K1, ZZ = range(8)

            def c_features(g, u):
                act.wait_ge(ln_xT, 2 * NG + g + 1)
                wait(act, c_kv, g - 1)
                act.activation(xF[:, u, :], bank(T_, P, FC), ACT.Identity, bias=c_b1[:, :], scale=c_g1[:, :]).then_inc(ln_xF, 1)

            def c_kvs(g, u):
                act.wait_ge(c_kv, g + 1)
                wait(act, c_sy, g - 1)
                copy_out(kS[:, u, :], PS[:, A_, 0:FC])
                copy_out(ukS[:, u, :], PS[:, A_, 0:FC], bias=c_u[:, :])
                copy_out(vS[:, u, :], PS[:, A_, FC:2 * FC])
                act.activation(rS[:, u, :], PS[:, R_, 0:FC], ACT.Tanh, scale=0.5).then_inc(c_kvS, 1)

            def c_exps(g, u):
                act.wait_ge(c_arg, g + 1)
                wait(act, c_sy, g)
                act.activation(ex[:, :, :], arg[:, :, :], ACT.Exp).then_inc(c_exp, 1)

            def c_features2(g, u):
                act.wait_ge(c_xT2, g + 1)
                wait(act, c_ff, g)
                act.activation(h2F[:, :], bank(T2, P, FC), ACT.Identity, bias=c_b2[:, :], scale=c_g2[:, :]).then_inc(c_h2F, 1)

            def c_relu2(g, u):
                act.wait_ge(c_ff, g + 1)
                wait(act, c_vfd, g)
                wait(act, c_h, g)
                act.activation(kr[:, :, :], PS[:, K0:K1 + 1, 0:G * NTOK], ACT.Relu).then_inc(c_krS, 1)
                act.activation(r2S[:, :], PS[0:NTOK, ZZ, 0:GC], ACT.Tanh, scale=0.5).then_inc(c_r2S, 1)
                act.wait_ge(c_krS, g + 1)
                act.activation(kk2[:, :, :], kr[:, :, :], ACT.Square).then_inc(c_kkS, 1)

            grouped(act, NG, (1, c_features), (3, c_features2), (1, c_kvs), (3, c_relu2), (2, c_exps))

            act.wait_ge(c_h, NG)

            def d_features(g, u):
                act.wait_ge(ln_xT, 3 * NG + g + 1)
                wait(act, d_lg, g - 1)
                copy_out(xF[:, u, :], bank(0, P, FC)).then_inc(ln_xF, 1)

            def d_logitsS(g, u):
                act.wait_ge(d_lg, g + 1)
                wait(act, d_i8, (g - 1) * G)
                copy_out(Lg[:, u, :, :], bank(1, NTOK, G * NX).rearrange("p (b e) -> p b e", b=G)).then_inc(d_lgS, 1)

            grouped(act, NG, (1, d_features), (1, d_logitsS))
            act.wait_ge(d_diff, 1)
            act.activation(TV[:, 1, :], TV[:, 1, :], ACT.Exp).then_inc(d_exp, 1)

            def e_rows(g, u):
                act.wait_ge(e_xT, g + 1)
                wait(act, e_up, g - 1)
                copy_out(xT[0:D, u % 2, :], bank(u % 2, D, EB * SLOT)).then_inc(e_xTs, 1)

            def e_out(g, u):
                act.wait_ge(e_down, g + 1)
                wait(act, e_st[u % 2], (g - u % 2) * 8)
                copy_out(yb[:, u % 2, :, :], bank(4 + u % 2, P, EB * D).rearrange("p (k d) -> p k d", k=EB)).then_inc(e_y, 1)

            grouped(act, NBLK // EB, (0, e_rows), (2, e_out), unroll=4)

        @block.gpsimd
        def _(pool):
            for tile in zeroed:
                pool.memset(tile[:], 0.0).then_inc(zeros_set, 1)
            pool.memset(zt[:, :], 0.0).then_inc(zeros_set, 1)
            pool.memset(onesq[:, :], 1.0).then_inc(const_set, 1)
            pool.memset(d_oneb[:, :], 1.0).then_inc(const_set, 1)
            pool.memset(ones[:, :], 1.0).then_inc(const_set, 1)
            pool.memset(mhalf[:, :], -0.5).then_inc(const_set, 1)
            pool.memset(Vx[:, :, :, :].rearrange("p a b c -> p (a b c)"), 1.0).then_inc(const_set, 1)
            pool.memset(cmask[:, :, :].rearrange("p a b -> p (a b)"), 0.0).then_inc(const_set, 1)
            pool.memset(identb[:, :], 1.0).then_inc(const_set, 1)
            pool.wait_ge(const_set, 7)
            pool.affine_select(out=cmask[:, :, :], in_=cmask[:, :, :], compare_op=ALU.is_ge, fill=-1e30, base=0,
                               pattern=[[0, NE], [-1, NTOK]], channel_multiplier=1).then_inc(mask_set, 1)
            pool.affine_select(out=identb[:, :], in_=identb[:, :], compare_op=ALU.is_equal, fill=0.0, base=0,
                               pattern=[[-1, NTOK]], channel_multiplier=1).then_inc(mask_set, 1)
            pool.wait_ge(rope_set, 1)

            def a_power(g, u):
                pool.wait_ge(ln_var, g + 1)
                wait(pool, ln_xn, g - 1)
                pool.tensor_tensor(rstd[0:NTOK, u, 0:G], stat[0:NTOK, u, 2, 0:G], mhalf[0:NTOK, 0:G],
                                   ALU.pow).then_inc(ln_rstd, 1)

            def a_kparts(g, u):
                pool.wait_ge(a_silu, g * 4 + 2)
                wait(pool, a_rope, g - 1)
                for dst, src, tab in ((ka, Bs, rk[0]), (kb, Bw, rk[1])):
                    pool.tensor_tensor(dst[:, u, :].rearrange("p (b t) -> p b t", b=G),
                                       src[:, u, :].rearrange("p (b t) -> p b t", b=G),
                                       tab[:, :].unsqueeze(1).broadcast_to([P, G, NTOK]), ALU.mult).then_inc(a_kpart, 1)

            grouped(pool, NG, (0, a_power), (1, a_kparts))

            pool.wait_ge(a_h, NG)

            def b_power(g, u):
                pool.wait_ge(ln_var, NG + g + 1)
                wait(pool, ln_xn, NG + g - 1)
                pool.tensor_tensor(rstd[0:NTOK, u, 0:G], stat[0:NTOK, u, 2, 0:G], mhalf[0:NTOK, 0:G],
                                   ALU.pow).then_inc(ln_rstd, 1)

            def b_pads(b):
                def stage(g, u):
                    pool.wait_ge(b_oc, (g * G + b) * 2 + 2)
                    pool.wait_ge(b_pad, g + 1)
                    o = OT[:, u, b, :].rearrange("p (n e d) -> p n e d", n=NH, e=NE)
                    m = padm[:, u, b * D:(b + 1) * D].rearrange("p (n d) -> p n d", n=NH)
                    pool.tensor_tensor(o, o, m.unsqueeze(2).broadcast_to([NTOK, NH, NE, DH]),
                                       ALU.mult).then_inc(b_om, 1)
                return stage

            def b_weigh(g, u):
                pool.wait_ge(b_gs, g + 1)
                wait(pool, b_pw1, g)
                pool.tensor_tensor(M1[:, :].rearrange("p (m d) -> p m d", d=DH),
                                   OT[:, u, :, :].rearrange("p b (m d) -> p (b m) d", d=DH),
                                   gs[:, :].unsqueeze(2).broadcast_to([NTOK, G * NM, DH]), ALU.mult).then_inc(b_m1, 1)

            def b_pow1(g, u):
                pool.wait_ge(b_pw1, g + 1)
                pool.tensor_tensor(hst[:, 3, :], hst[:, 2, :], mhalf[0:NTOK, :], ALU.pow).then_inc(b_r1, 1)

            def b_pow2(g, u):
                pool.wait_ge(b_pw2, g + 1)
                pool.tensor_tensor(hst[:, 3, :], hst[:, 2, :], mhalf[0:NTOK, :], ALU.pow).then_inc(b_r2, 1)

            grouped(pool, NG, (0, b_power), (3, b_weigh), (3, b_pow1), (2, b_pads(0)), (2, b_pads(1)),
                    (3, b_pow2), (2, b_pads(2)), (2, b_pads(3)))

            pool.wait_ge(b_h, NG)

            def c_power(g, u):
                pool.wait_ge(ln_var, 2 * NG + g + 1)
                wait(pool, ln_xn, 2 * NG + g - 1)
                pool.tensor_tensor(rstd[0:NTOK, u, :], stat[0:NTOK, u, 2, :], mhalf[0:NTOK, 0:2 * G],
                                   ALU.pow).then_inc(ln_rstd, 1)

            def c_power2(g, u):
                pool.wait_ge(c_var2, g + 1)
                wait(pool, c_xn2, g - 1)
                pool.tensor_tensor(hst2[:, u, G:2 * G], hst2[:, u, 0:G], mhalf[0:NTOK, 0:G], ALU.pow).then_inc(c_rstd2, 1)

            grouped(pool, NG, (0, c_power), (2, c_power2))

            pool.wait_ge(c_h, NG)

            def d_power(g, u):
                pool.wait_ge(ln_var, 3 * NG + g + 1)
                wait(pool, ln_xn, 3 * NG + g - 1)
                pool.tensor_tensor(rstd[0:NTOK, u, 0:G], stat[0:NTOK, u, 2, 0:G], mhalf[0:NTOK, 0:G],
                                   ALU.pow).then_inc(ln_rstd, 1)

            def d_keep(g, u):
                pool.wait_ge(ln_xn, 3 * NG + g + 1)
                pool.tensor_copy(XR[0:NTOK, ds(g * GC, GC)], xn[0:NTOK, u, :]).then_inc(d_xr, 1)

            grouped(pool, NG, (0, d_power), (1, d_keep))

            pool.wait_ge(zeros_out, 16 * (NBLK * SLOT * D // (P * 1024)))
            pool.wait_ge(d_slots, 1)
            pool.wait_ge(d_xr, NG)
            for b in range(B):
                for k in range(2):
                    pool.indirect_dma_start(XD, bass.IndirectOffsetOnAxis(SLu[:, k, b:b + 1], 0),
                                            XR[0:NTOK, b * D:(b + 1) * D], None).then_inc(scat, 16)
            pool.wait_ge(scat, 16 * 2 * B)
            for st in e_st:
                pool.wait_ge(st, 16 * (NBLK // EB // 2))
            for b in range(B):
                for k, dst in enumerate((XR, Y2g)):
                    pool.indirect_dma_start(dst[0:NTOK, b * D:(b + 1) * D], None, YD,
                                            bass.IndirectOffsetOnAxis(SLu[:, k, b:b + 1], 0)).then_inc(gath[b // CH], 16)

        @block.vector
        def _(dve):
            dve.wait_ge(weights_in, 16 * len(loads))
            n = 0
            for (w, b_), (ws, bs_), (t0, t1, t2) in (((a_qk[0], a_qk[1]), (a_qks[0], a_qks[1]), rq),
                                                    ((a_qk[2], a_qk[3]), (a_qks[2], a_qks[3]), rk)):
                dve.tensor_scalar(t0[:, :], ropec[:, :], w[:, 0:1], None, ALU.mult)
                dve.tensor_scalar(t1[:, :], ropes[:, :], ws[:, 0:1], None, ALU.mult)
                dve.tensor_scalar(rt[:, 0, :], ropec[:, :], b_[:, 0:1], None, ALU.mult).then_inc(rope_chain, 1)
                n += 1
                dve.wait_ge(rope_chain, n)
                dve.scalar_tensor_tensor(t2[:, :], ropes[:, :], bs_[:, 0:1], rt[:, 0, :], ALU.mult,
                                         ALU.add).then_inc(rope_chain, 1)
                n += 1
                dve.wait_ge(rope_chain, n)
            dve.wait_ge(wrep_done, 1)
            dve.tensor_copy(wrep[:, :], bank(4, P, D)).then_inc(rope_chain, 1)
            dve.wait_ge(rope_chain, n + 1)
            for j in range(GRID):
                dve.tensor_scalar(gsel[:, j, :], wrep[:, :], jmask[:, j:j + 1], None, ALU.mult).then_inc(gsel_done, 1)
            dve.wait_ge(hank_done, 1)
            dve.tensor_copy(biasT[:, :], bank(5, NTOK, NTOK)).then_inc(rope_set, 1)
            dve.wait_ge(rope_set, 1)
            dve.wait_ge(tokT_kept, B // 8)
            dve.wait_ge(txt_in, 16)

            K_, O_, W_ = 5, 6, 7

            def a_ln(g, u):
                wait(dve, ln_rstd, g - 1)
                ln_sums(dve, g, u, 0)
                dve.tensor_scalar(stat[0:NTOK, u, 2, 0:G], stat[0:NTOK, u, 0, 0:G], (1 + EPS5) / D,
                                  EPS5 * EPS5, ALU.mult, ALU.add).then_inc(ln_var, 1)

            def a_norm(g, u):
                dve.wait_ge(ln_rstd, g + 1)
                wait(dve, ln_xT, g - 1)
                dve.tensor_tensor(xn[0:NTOK, u, :].rearrange("p (b d) -> p b d", d=D),
                                  xc[0:NTOK, u, :].rearrange("p (b d) -> p b d", d=D),
                                  rstd[0:NTOK, u, 0:G].unsqueeze(2).broadcast_to([NTOK, G, D]),
                                  ALU.mult).then_inc(ln_xn, 1)

            def a_ropes(g, u):
                def v(t):
                    return t[:, u, :].rearrange("p (b t) -> p b t", b=G)

                def tab(t):
                    return t[:, :].unsqueeze(1).broadcast_to([P, G, NTOK])
                c = g * 5
                dve.wait_ge(a_silu, g * 4 + 2)
                wait(dve, a_qk_done, g - 1)
                dve.tensor_tensor(v(qa), v(Bs), tab(rq[0]), ALU.mult).then_inc(a_ropec, 1)
                dve.tensor_tensor(v(qb), v(Bw), tab(rq[1]), ALU.mult).then_inc(a_ropec, 1)
                dve.wait_ge(a_kpart, g * 2 + 2)
                dve.tensor_tensor(ka[:, u, :], ka[:, u, :], kb[:, u, :], ALU.add).then_inc(a_ropec, 1)
                dve.wait_ge(a_ropec, c + 2)
                dve.tensor_tensor(qa[:, u, :], qa[:, u, :], qb[:, u, :], ALU.add).then_inc(a_ropec, 1)
                dve.wait_ge(a_ropec, c + 3)
                dve.tensor_tensor(v(ka), v(ka), tab(rk[2]), ALU.add).then_inc(a_ropec, 1)
                dve.wait_ge(a_ropec, c + 5)
                dve.tensor_tensor(v(qa), v(qa), tab(rq[2]), ALU.add).then_inc(a_rope, 1)

            def a_kernel(g, u):
                dve.wait_ge(a_qk_done, g + 1)
                wait(dve, a_av, g - 1)
                dve.scalar_tensor_tensor(za[0:NTOK, u, :].rearrange("p (b t) -> p b t", b=G),
                                         bank(K_, NTOK, G * NTOK).rearrange("p (b t) -> p b t", b=G), 1.0 / mpe,
                                         biasT[:, :].unsqueeze(1).broadcast_to([NTOK, G, NTOK]),
                                         ALU.mult, ALU.add).then_inc(a_kernc, 1)
                dve.wait_ge(a_kernc, g + 1)
                dve.scalar_tensor_tensor(KT[0:NTOK, u, :], za[0:NTOK, u, :], 0.0, za[0:NTOK, u, :],
                                         ALU.max, ALU.mult).then_inc(a_kern, 1)

            def a_gate(g, u):
                dve.wait_ge(a_av, g + 1)
                dve.wait_ge(a_silu, g * 4 + 3)
                wait(dve, a_wo_done, g - 1)
                dve.tensor_tensor(UO[:, u, :], bank(O_, P, G * NTOK), U[:, u, :], ALU.mult).then_inc(a_uo, 1)

            def a_residual(g, u):
                dve.wait_ge(a_wo_done, g + 1)
                dve.tensor_tensor(hgroup(g), bank(W_, NTOK, GC), hgroup(g), ALU.add).then_inc(a_h, 1)

            grouped(dve, NG, (2, a_ropes), (0, a_ln), (2, a_kernel), (0, a_norm), (2, a_gate), (2, a_residual))

            dve.wait_ge(a_h, NG)
            O_, F_, Q_, Z_ = 4, 5, 6, 7

            def b_ln(g, u):
                wait(dve, ln_rstd, NG + g - 1)
                ln_sums(dve, g, u, 1)
                dve.tensor_scalar(stat[0:NTOK, u, 2, 0:G], stat[0:NTOK, u, 0, 0:G], 1.0 / D, EPS5,
                                  ALU.mult, ALU.add).then_inc(ln_var, 1)

            def b_norm(g, u):
                dve.wait_ge(ln_rstd, NG + g + 1)
                wait(dve, ln_xT, NG + g - 1)
                dve.tensor_tensor(xn[0:NTOK, u, :].rearrange("p (b d) -> p b d", d=D),
                                  xc[0:NTOK, u, :].rearrange("p (b d) -> p b d", d=D),
                                  rstd[0:NTOK, u, 0:G].unsqueeze(2).broadcast_to([NTOK, G, D]),
                                  ALU.mult).then_inc(ln_xn, 1)

            def b_padmask(g, u):
                dve.wait_ge(b_vs, g + 1)
                wait(dve, b_om, (g - 1) * G)
                if isinstance(g, int) and g == 0:
                    dg = bass.AP(PS, PS[0:NTOK, F_, GC:GC + 1].offset,
                                 [[8 * 512, NTOK], [D + DH, NH], [1, DH]])
                    dve.tensor_copy(resid.rearrange("p (n d) -> p n d", n=NH), dg)
                dve.tensor_scalar(padm[:, u, :], PS[0:NTOK, F_, GC:2 * GC], 0.0, None,
                                  ALU.not_equal).then_inc(b_pad, 1)

            def b_slots(k0, k1):
                def stage(g, u):
                    for k in range(k0, k1):
                        if k < NU:
                            s = bank(k % 2, NTOK, NE * NTOK).rearrange("p (e t) -> p e t", e=NE)
                            dve.wait_ge(b_s, g * NU + (k + 1))
                            dve.tensor_reduce(mx[:, k % 2, :], s, AX_X, ALU.max).then_inc(b_max, 1)
                            dve.wait_ge(b_max, g * NU + (k + 1))
                            wait(dve, b_exp, g * NU + (k - 1))
                            dve.tensor_tensor(Pm[:, k % 2, :].rearrange("p (e t) -> p e t", e=NE), s,
                                              mx[:, k % 2, :].unsqueeze(2).broadcast_to([NTOK, NE, NTOK]),
                                              ALU.subtract).then_inc(b_sub, 1)
                        if k >= 6 and (k - 6) % 4 == 0:
                            b = (k - 6) // 4
                            o = bank(O_, NTOK, NM * (DH + 1)).rearrange("p (m d) -> p m d", m=NM)
                            dve.wait_ge(b_av, g * NU + 4 * b + 4)
                            dve.reciprocal(oden[:, :], o[:, :, DH]).then_inc(b_oc, 1)
                            dve.wait_ge(b_oc, (g * G + b) * 2 + 1)
                            if b == 0:
                                wait(dve, b_m1, g - 1)
                            ins = dve.tensor_tensor(OT[:, u, b, :].rearrange("p (m d) -> p m d", m=NM), o[:, :, 0:DH],
                                                    oden[:, :].unsqueeze(2).broadcast_to([NTOK, NM, DH]), ALU.mult)
                            ins.then_inc(b_oc, 1)
                            dve.wait_ge(b_oc, (g * G + b) * 2 + 2)
                            dve.sem_inc(b_o, 1)
                return stage

            def groups_of(t, n):
                return t.rearrange("p (m d) -> p m d", m=n)

            def wide(s, n, w):
                return s.unsqueeze(2).broadcast_to([NTOK, n, w])
            NS = G * NH

            def b_gate1(g, u):
                dve.wait_ge(b_gate, g + 1)
                z = groups_of(bank(Z_, NTOK, G * NM), NS)
                link = Link(dve, b_chain, g, B_LINKS, 0)
                link(dve.tensor_reduce(gst[:, 0, :], z, AX_X, ALU.max))
                dve.tensor_tensor(groups_of(gd[:, :], NS), z, wide(gst[:, 0, :], NS, NE), ALU.subtract).then_inc(b_gd, 1)

            def b_gate2(g, u):
                dve.wait_ge(b_ge, g + 1)
                wait(dve, b_m1, g)
                link = Link(dve, b_chain, g, B_LINKS, 1)
                link(dve.tensor_reduce(gst[:, 1, :], groups_of(ge[:, :], NS), AX_X, ALU.add))
                link(dve.reciprocal(gst[:, 2, :], gst[:, 1, :]))
                dve.tensor_tensor(groups_of(gs[:, :], NS), groups_of(ge[:, :], NS), wide(gst[:, 2, :], NS, NE),
                                  ALU.mult).then_inc(b_gs, 1)

            def head_ln_sums(src, link):
                link(dve.tensor_reduce(hst[:, 0, :], src, AX_X, ALU.add))
                link(dve.tensor_scalar(hst[:, 1, :], hst[:, 0, :], -1.0 / DH, None, ALU.mult))
                link(dve.tensor_tensor(groups_of(hc[:, :], NS), src, wide(hst[:, 1, :], NS, DH), ALU.add))
                link(dve.tensor_tensor(hs[:, :], hc[:, :], hc[:, :], ALU.mult))
                link(dve.tensor_reduce(hst[:, 0, :], groups_of(hs[:, :], NS), AX_X, ALU.add))
                return dve.tensor_scalar(hst[:, 2, :], hst[:, 0, :], 1.0 / DH, EPS8, ALU.mult, ALU.add)

            def head_ln_end(dst, gain, shift, link):
                def row(w):
                    return w[:, :].unsqueeze(1).broadcast_to([NTOK, NS, DH])
                link(dve.tensor_tensor(groups_of(hs[:, :], NS), groups_of(hc[:, :], NS), wide(hst[:, 3, :], NS, DH), ALU.mult))
                link(dve.tensor_tensor(groups_of(hs[:, :], NS), groups_of(hs[:, :], NS), row(gain), ALU.mult))
                return dve.tensor_tensor(groups_of(dst, NS), groups_of(hs[:, :], NS), row(shift), ALU.add)

            def b_mix(g, u):
                dve.wait_ge(b_m1, g + 1)
                link = Link(dve, b_chain, g, B_LINKS, 3)
                m = M1[:, :].rearrange("p (s e d) -> p s d e", s=NS, e=NE)
                link(dve.tensor_reduce(groups_of(hm[:, :], NS), m, AX_X, ALU.add))
                link(dve.tensor_tensor(hm[:, :].rearrange("p (b d) -> p b d", b=G), hm[:, :].rearrange("p (b d) -> p b d", b=G),
                                       resid[:, :].unsqueeze(1).broadcast_to([NTOK, G, D]), ALU.add))
                link = Link(dve, b_chain, g, B_LINKS, 5)
                head_ln_sums(groups_of(hm[:, :], NS), link).then_inc(b_pw1, 1)

            def b_hns(g, u):
                dve.wait_ge(b_r1, g + 1)
                link = Link(dve, b_chain, g, B_LINKS, 10)
                head_ln_end(hn[:, :], f_aff[0], f_aff[1], link).then_inc(b_hn, 1)

            def b_h1s(g, u):
                dve.wait_ge(b_fc1, g + 1)
                dve.tensor_scalar(pmF[:, :], fxF[:, :], 0.0, None, ALU.not_equal)
                link = Link(dve, b_chain, g, B_LINKS, 12)
                link(dve.tensor_scalar(h1[:, :], bank(Z_, P, FC), f_b1[:, 0:1], 0.0, ALU.add, ALU.max))
                dve.tensor_tensor(h1[:, :], h1[:, :], pmF[:, :], ALU.mult).then_inc(b_h1, 1)

            def b_ys(g, u):
                dve.wait_ge(b_fc2, g + 1)
                link = Link(dve, b_chain, g, B_LINKS, 13)
                link(dve.scalar_tensor_tensor(yF[:, :], bank(Z_, P, FC), f_b2[:, 0:1], pmF[:, :], ALU.add, ALU.mult))
                dve.tensor_tensor(yF[:, :], yF[:, :], fxF[:, :], ALU.add).then_inc(b_y, 1)

            def b_ln2(g, u):
                dve.wait_ge(b_yT, g + 1)
                link = Link(dve, b_chain, g, B_LINKS, 14)
                head_ln_sums(groups_of(bank(Z_, NTOK, GC), NS), link).then_inc(b_pw2, 1)

            def b_fos(g, u):
                dve.wait_ge(b_r2, g + 1)
                link = Link(dve, b_chain, g, B_LINKS, 19)
                head_ln_end(fo[:, :], f_aff[2], f_aff[3], link).then_inc(b_fo, 1)

            def b_w1(g, u):
                dve.wait_ge(b_fg, g + 1)
                z = groups_of(bank(Z_, NTOK, NS), G)
                link = Link(dve, b_chain, g, B_LINKS, 21)
                link(dve.tensor_reduce(gst[:, 0, 0:G], z, AX_X, ALU.max))
                link(dve.tensor_tensor(groups_of(gd[:, 0:NS], G), z, wide(gst[:, 0, 0:G], G, NH), ALU.subtract))
                dve.sem_inc(b_wd, 1)

            def b_w2(g, u):
                dve.wait_ge(b_we, g + 1)
                link = Link(dve, b_chain, g, B_LINKS, 23)
                link(dve.tensor_reduce(gst[:, 1, 0:G], groups_of(ge[:, 0:NS], G), AX_X, ALU.add))
                link(dve.reciprocal(gst[:, 2, 0:G], gst[:, 1, 0:G]))
                link(dve.tensor_tensor(groups_of(gst[:, 3, :], G), groups_of(ge[:, 0:NS], G),
                                       wide(gst[:, 2, 0:G], G, NH), ALU.mult))
                link(dve.tensor_tensor(groups_of(hs[:, :], NS), groups_of(fo[:, :], NS), wide(gst[:, 3, :], NS, DH), ALU.mult))
                dve.tensor_tensor(hgroup(g), hgroup(g), hs[:, :], ALU.add).then_inc(b_h, 1)

            grouped(dve, NG, (2, b_slots(0, 2)), (3, b_gate1), (0, b_ln), (2, b_slots(2, 3)), (3, b_gate2),
                    (2, b_slots(3, 4)), (0, b_norm), (1, b_padmask), (2, b_slots(4, 6)), (3, b_mix),
                    (2, b_slots(6, 7)), (3, b_hns), (2, b_slots(7, 8)), (3, b_h1s), (2, b_slots(8, 9)), (3, b_ys),
                    (2, b_slots(9, 11)), (3, b_ln2), (2, b_slots(11, 13)), (3, b_fos), (2, b_slots(13, 15)),
                    (3, b_w1), (2, b_slots(15, 17)), (3, b_w2), (2, b_slots(17, 19)))

            dve.wait_ge(b_h, NG)
            T_, A_, R_, OO, T2, K0, K1, ZZ = range(8)
            link = Link(dve, c_tab, 0, 5)
            first = c_start[:, :].rearrange("p (q t) -> p q t", q=2)[:, :, 0]
            link(dve.memset(c_start[:, :], 0.0))
            link(dve.memset(first, -1e38))
            link(dve.tensor_scalar(c_w[:, :], c_w[:, :], 1.0 / NTOK, None, ALU.mult))
            link(dve.tensor_scalar(c_u[:, :], c_u[:, :], 1.0 / NTOK, None, ALU.mult))
            dve.memset(Os[:, 0:1], -1e38).then_inc(tab_set, 1)
            dve.memset(Qs[:, 0:1], 0.0).then_inc(tab_set, 1)
            dve.memset(Ns[:, 0:1], 0.0).then_inc(tab_set, 1)
            link(dve.tensor_scalar(c_decay[:, :], c_start[:, :], c_w[:, 0:1], None, ALU.add))
            dve.wait_ge(tab_set, 3)

            def rows_of(t):
                return t.rearrange("p (b d) -> p b d", d=D)

            def c_ln(g, u):
                wait(dve, ln_rstd, 2 * NG + g - 1)
                ln_sums(dve, g, u, 2)
                s_ = stat[0:NTOK, u, 0, 0:G]
                dve.tensor_scalar(stat[0:NTOK, u, 2, 0:G], s_, 1.0 / D, EPS5, ALU.mult, ALU.add)
                dve.tensor_scalar(stat[0:NTOK, u, 2, G:2 * G], s_, (1 + EPS5) / D, EPS5 * EPS5,
                                  ALU.mult, ALU.add).then_inc(ln_var, 1)

            def c_norm(g, u):
                dve.wait_ge(ln_rstd, 2 * NG + g + 1)
                wait(dve, ln_xT, 2 * NG + g - 1)
                for dst, k, done in ((xn[0:NTOK, u, :], G, ln_xn), (X1[:, u, :], 0, c_x1)):
                    dve.tensor_tensor(rows_of(dst), rows_of(xc[0:NTOK, u, :]),
                                      rstd[0:NTOK, u, k:k + G].unsqueeze(2).broadcast_to([NTOK, G, D]),
                                      ALU.mult).then_inc(done, 1)

            def c_wkv1(g, u):
                dve.wait_ge(c_kvS, g + 1)
                wait(dve, c_exp, g)
                link = Link(dve, c_chain, g, C_LINKS, 0)
                k, uk = kS[:, u, :], ukS[:, u, :]
                link(dve.tensor_tensor_scan(Os[:, 1:FC + 1], c_decay[:, :], k, -1e38, ALU.add, ALU.max))
                link(dve.tensor_tensor(Oq[:, :], Os[:, 0:FC], c_start[:, :], ALU.add))
                dve.tensor_tensor(arg[:, 3, :], k, Os[:, 1:FC + 1], ALU.subtract)
                dve.scalar_tensor_tensor(arg[:, 2, :], Oq[:, :], c_w[:, 0:1], Os[:, 1:FC + 1], ALU.add, ALU.subtract)
                link(dve.tensor_tensor(no[:, :], Oq[:, :], uk, ALU.max))
                dve.tensor_tensor(arg[:, 0, :], Oq[:, :], no[:, :], ALU.subtract)
                dve.tensor_tensor(arg[:, 1, :], uk, no[:, :], ALU.subtract).then_inc(c_arg, 1)

            def c_wkv2(g, u):
                dve.wait_ge(c_exp, g + 1)
                wait(dve, c_wod, g)
                v = vS[:, u, :]
                link = Link(dve, c_chain, g, C_LINKS, 3)
                dve.tensor_tensor_scan(Qs[:, 1:FC + 1], ex[:, 2, :], ex[:, 3, :], 0.0, ALU.mult, ALU.add)
                link(dve.tensor_tensor(w1[:, :], ex[:, 3, :], v, ALU.mult))
                dve.tensor_tensor(w2[:, :], ex[:, 0, :], Qs[:, 0:FC], ALU.mult)
                link(dve.tensor_tensor_scan(Ns[:, 1:FC + 1], ex[:, 2, :], w1[:, :], 0.0, ALU.mult, ALU.add))
                dve.tensor_tensor(w3[:, :], ex[:, 1, :], v, ALU.mult)
                link(dve.tensor_tensor(w2[:, :], w2[:, :], ex[:, 1, :], ALU.add))
                link(dve.tensor_tensor(w4[:, :], ex[:, 0, :], Ns[:, 0:FC], ALU.mult))
                link(dve.reciprocal(w1[:, :], w2[:, :]))
                dve.tensor_tensor(w3[:, :], w3[:, :], w4[:, :], ALU.add)
                link(dve.scalar_tensor_tensor(w2[:, :], rS[:, u, :], 1.0, w1[:, :], ALU.add, ALU.mult))
                dve.tensor_tensor(sy[:, :], w3[:, :], w2[:, :], ALU.mult).then_inc(c_sy, 1)

            def c_resid(g, u):
                dve.wait_ge(c_wod, g + 1)
                dve.wait_ge(c_x1, g + 1)
                dve.scalar_tensor_tensor(X2[:, u, :], PS[0:NTOK, OO, 0:GC], 0.5, X1[:, u, :], ALU.mult,
                                         ALU.add).then_inc(c_x2, 1)
                dve.wait_ge(c_x2, g + 1)
                wait(dve, c_rstd2, g - 1)
                s_, m_ = hst2[:, u, 0:G], hst2[:, u, G:2 * G]
                v, c3 = rows_of(X2[:, u, :]), rows_of(hc2[:, u, :])
                link = Link(dve, c_chain, g, C_LINKS, 9)
                link(dve.tensor_reduce(s_, v, AX_X, ALU.add))
                link(dve.tensor_scalar(m_, s_, -1.0 / D, None, ALU.mult))
                link(dve.tensor_tensor(c3, v, m_.unsqueeze(2).broadcast_to([NTOK, G, D]), ALU.add))
                link(dve.tensor_tensor(fT[:, :], hc2[:, u, :], hc2[:, u, :], ALU.mult))
                link(dve.tensor_reduce(s_, rows_of(fT[:, :]), AX_X, ALU.add))
                dve.tensor_scalar(s_, s_, 1.0 / D, EPS5, ALU.mult, ALU.add).then_inc(c_var2, 1)

            def c_norm2(g, u):
                dve.wait_ge(c_rstd2, g + 1)
                wait(dve, c_xT2, g - 1)
                dve.tensor_tensor(rows_of(xn2[:, u, :]), rows_of(hc2[:, u, :]),
                                  hst2[:, u, G:2 * G].unsqueeze(2).broadcast_to([NTOK, G, D]), ALU.mult).then_inc(c_xn2, 1)

            def c_end(g, u):
                dve.wait_ge(c_vfd, g + 1)
                link = Link(dve, c_fc, g, 3)
                link(dve.scalar_tensor_tensor(fT2[:, :], r2S[:, :], 1.0, PS[0:NTOK, ZZ, GC:2 * GC], ALU.add, ALU.mult))
                link(dve.scalar_tensor_tensor(fT2[:, :], fT2[:, :], 0.5, X2[:, u, :], ALU.mult, ALU.add))
                link(dve.tensor_tensor(hgroup(g), hgroup(g), fT2[:, :], ALU.add))
                dve.sem_inc(c_h, 1)

            grouped(dve, NG, (2, c_wkv1), (0, c_ln), (2, c_wkv2), (3, c_end), (2, c_resid), (0, c_norm), (2, c_norm2))

            dve.wait_ge(c_h, NG)

            def d_ln(g, u):
                wait(dve, ln_rstd, 3 * NG + g - 1)
                ln_sums(dve, g, u, 3)
                dve.tensor_scalar(stat[0:NTOK, u, 2, 0:G], stat[0:NTOK, u, 0, 0:G], 1.0 / D, EPS5,
                                  ALU.mult, ALU.add).then_inc(ln_var, 1)

            def d_norm(g, u):
                dve.wait_ge(ln_rstd, 3 * NG + g + 1)
                wait(dve, ln_xT, 3 * NG + g - 1)
                wait(dve, d_xr, g - 1)
                dve.tensor_tensor(rows_of(xn[0:NTOK, u, :]), rows_of(xc[0:NTOK, u, :]),
                                  rstd[0:NTOK, u, 0:G].unsqueeze(2).broadcast_to([NTOK, G, D]), ALU.mult).then_inc(ln_xn, 1)

            def d_best(g, u):
                dve.wait_ge(d_lgS, g + 1)
                dve.sem_inc(d_go, 1)
                for b in range(G):
                    dve.max(out=m8[:, u, b, :], in_=Lg[:, u, b, :]).then_inc(d_m8, 1)
                dve.wait_ge(d_m8, g * G + G)
                dve.sem_inc(d_go, 1)
                for b in range(G):
                    dve.max_index(out=i8[:, u, b, :], in_max=m8[:, u, b, :], in_values=Lg[:, u, b, :]).then_inc(d_i8, 1)
                dve.tensor_copy(TV[:, :, ds(g * G, G)], m8[:, u, :, 0:2].rearrange("p b k -> p k b")).then_inc(d_top, 1)
                dve.wait_ge(d_i8, g * G + G)
                dve.tensor_copy(TI[:, :, ds(g * G, G)], i8[:, u, :, 0:2].rearrange("p b k -> p k b")).then_inc(d_top, 1)

            grouped(dve, NG, (2, d_best), (0, d_ln), (0, d_norm))
            dve.wait_ge(d_top, 2 * NG)
            dve.tensor_copy(d_trib[:, :], d_tri[:, :]).then_inc(d_oh, 1)
            dve.tensor_tensor(TV[:, 1, :], TV[:, 1, :], TV[:, 0, :], ALU.subtract).then_inc(d_diff, 1)

            def seq(t):
                return t.rearrange("p (b e) -> p b e", e=NX)
            iota = d_iota[:, 0:NX].unsqueeze(1).broadcast_to([NTOK, B, NX])
            link = Link(dve, d_chain, 0, D_LINKS)
            for k, oh in enumerate((OH1, OH2)):
                link(dve.tensor_tensor(seq(oh[:, :]), TI[:, k, :].unsqueeze(2).broadcast_to([NTOK, B, NX]), iota, ALU.is_equal))
            dve.tensor_tensor(OHs[:, :], OH1[:, :], OH2[:, :], ALU.add).then_inc(d_oh, 2)
            dve.wait_ge(d_exp, 1)
            link(dve.tensor_scalar(TV[:, 0, :], TV[:, 1, :], 1.0, None, ALU.add))
            link(dve.reciprocal(TV[:, 0, :], TV[:, 0, :]))
            link(dve.tensor_tensor(TV[:, 1, :], TV[:, 1, :], TV[:, 0, :], ALU.mult))
            dve.wait_ge(d_cnt, 1)
            link(dve.tensor_tensor_scan(cnt[:, 0, :], onesq[0:NX, 0:B], PS[0:NX, 2, 0:B], 0.0, ALU.mult, ALU.add))
            link(dve.tensor_tensor(cnt[:, 1, :], cnt[:, 0, :], PS[0:NX, 2, 0:B], ALU.subtract))
            link(dve.tensor_scalar(cmp[:, :], d_iota[0:NX, :], float(SLOT), cnt[:, 0, B - 1:B], ALU.mult, ALU.is_lt))
            dve.tensor_reduce(cs[:, 0:1], cmp[:, :], AX_X, ALU.add).then_inc(d_nblk, 1)
            dve.wait_ge(d_base, 1)
            link(dve.tensor_scalar(cs[:, 2:3], PS[0:NX, 3, 0:1], float(SLOT), None, ALU.mult))
            link(dve.tensor_tensor(cs[:, 3:4], PS[0:NX, 3, 0:1], cs[:, 0:1], ALU.add))
            dve.tensor_scalar(cmp[:, :], d_iota[0:NX, :], cs[:, 3:4], None, ALU.is_ge).then_inc(d_cmp, 1)
            link(dve.tensor_scalar(cnt[:, 2, :], cnt[:, 1, :], cs[:, 2:3], None, ALU.add))
            dve.tensor_tensor(seq(OD[0:NX, :]), cnt[:, 2, :].unsqueeze(2).broadcast_to([NX, B, NX]),
                              ident[0:NX, 0:NX].unsqueeze(1).broadcast_to([NX, B, NX]), ALU.mult).then_inc(d_off, 1)
            dve.wait_ge(d_blkp, 1)
            link(dve.tensor_scalar(blk[:, :], PS[0:1, 3, 0:NBLK], float(NX - 1), None, ALU.min))
            dve.tensor_copy(blku[:, :], blk[:, :]).then_inc(d_blk, 1)

            def d_slot(g, u):
                dve.wait_ge(d_rank, g + 1)
                link = Link(dve, d_chain, g, 4)
                link.base = D_LINKS + g * 4
                for k, oh in enumerate((OH1, OH2)):
                    pr = (xc, sq)[k][0:NTOK, :, :].rearrange("p a b -> p (a b)")
                    ins = dve.tensor_tensor(pr, bank(4 + u, NTOK, 512), oh[:, ds(g * 512, 512)], ALU.mult)
                    link(ins)
                    ins = dve.tensor_reduce(TS_[:, k, ds(g * 8, 8)], seq(pr), AX_X, ALU.add)
                    link(ins)
                dve.sem_inc(d_rankS, 1)
            grouped(dve, B // 8, (0, d_slot))
            dve.tensor_copy(SLu[:, :, :], TS_[:, :, :]).then_inc(d_slots, 1)

            dve.memset(xT[D:D + 1, 0, :], 1.0).then_inc(e_ones, 1)
            dve.memset(xT[D:D + 1, 1, :], 1.0).then_inc(e_ones, 1)

            def e_relu(g, u):
                dve.wait_ge(e_up, g + 1)
                wait(dve, e_down, g - 1)
                dve.tensor_scalar(hT[:, u % 2, :], bank(2 + u % 2, P, EB * SLOT), 0.0, None, ALU.max).then_inc(e_h, 1)
            grouped(dve, NBLK // EB, (1, e_relu), unroll=4)

            link = Link(dve, d_sum, 0, 2 * (B // CH))
            for c in range(B // CH):
                dve.wait_ge(gath[c], 16 * 2 * CH)
                t = slice(c * CH * D, (c + 1) * CH * D)
                gate = [TV[:, k, c * CH:(c + 1) * CH].unsqueeze(2).broadcast_to([NTOK, CH, D]) for k in range(2)]
                dve.tensor_tensor(rows_of(XR[0:NTOK, t]), rows_of(XR[0:NTOK, t]), gate[0], ALU.mult)
                link(dve.tensor_tensor(rows_of(Y2g[:, t]), rows_of(Y2g[:, t]), gate[1], ALU.mult))
                link(dve.tensor_tensor(XR[0:NTOK, t], XR[0:NTOK, t], Y2g[:, t], ALU.add))
                dve.tensor_tensor(H[:, t], H[:, t], XR[0:NTOK, t], ALU.add).then_inc(d_comb, 1)


def _bilinear(n_in, n_out):
    scale = n_out / n_in
    centre = (np.arange(n_out) + 0.5) / scale - 0.5
    w = np.maximum(0.0, 1.0 - np.abs(centre[:, None] - np.arange(n_in)[None, :]) * scale)
    return w / w.sum(1, keepdims=True)


def _constants():
    s = 0.7071067811865476

    def haar(n, sign):
        m = np.zeros((n // 2, n))
        m[np.arange(n // 2), 2 * np.arange(n // 2)] = s
        m[np.arange(n // 2), 2 * np.arange(n // 2) + 1] = sign * s
        return m
    lo1, hi1 = haar(IMG, 1), haar(IMG, -1)
    lo2, hi2 = haar(IMG // 2, 1), haar(IMG // 2, -1)
    r1, r2 = _bilinear(IMG // 2, GRID), _bilinear(IMG // 4, GRID)
    filt = np.concatenate([r2 @ lo2 @ lo1, r2 @ hi2 @ lo1, r1 @ lo1, r1 @ hi1])
    maps = [(0, 0), (1, 0), (0, 1), (1, 1), (3, 2), (2, 3), (3, 3)]
    sel = np.zeros((7, 4, 4, GRID))
    for m, (r, c) in enumerate(maps):
        sel[m, r, c] = 1
    half = E_ATT // 2
    inv = (10000.0 ** (-np.arange(half, dtype=np.float32) / np.float32(half))).astype(np.float32)
    ang = np.arange(NTOK, dtype=np.float32)[None, :] * inv[:, None]
    return {
        "c_tri": np.triu(np.ones((P, P)), 1), "c_iota": np.arange(NBLK),
        "c_ident": np.eye(P), "c_antid": np.eye(NTOK)[::-1], "c_filt": filt.T, "c_sel": sel.reshape(7, P),
        "c_jmask": (np.arange(P)[:, None] % GRID == np.arange(GRID)[None, :]),
        "c_cos": np.concatenate([np.cos(ang)] * 2), "c_sin": np.concatenate([-np.sin(ang), np.sin(ang)]),
    }


def kernel(**inputs):
    import concourse.bacc as bacc
    from concourse.bass_utils import run_bass_kernel_spmd
    nc = bacc.Bacc("TRN2", target_bir_lowering=False, num_devices=1)
    arrays, t_in = {}, {}
    turned = {"t_hl_w": ("L0_ffn_hl_w", (2, 0, 1), (D, D)), "t_fgate_w": ("L0_ffn_fgate_w", (1, 0), (D, NH)),
              "t_wq": ("L0_ffn_wq", (0, 3, 1, 2), (NH, DH, NE, DH)), "t_wk": ("L0_ffn_wk", (0, 2, 1), (NH, DH, DH)),
              "t_wv": ("L0_ffn_wv", (0, 2, 1), (NH, DH, DH)), "t_fc1_w": ("L0_ffn_fc1_w", (1, 0), (DH, DH)),
              "t_fc2_w": ("L0_ffn_fc2_w", (1, 0), (DH, DH)), "t_gate_w": ("L0_ffn_gate_w", (0, 2, 1), (NH, NE * DH, NE))}
    for name, (source, axes, shape) in turned.items():
        inputs[name] = np.ascontiguousarray(np.transpose(inputs[source], axes)).reshape(shape)
    for source in {v[0] for v in turned.values()}:
        del inputs[source]
    w1, b1, w2, b2 = (inputs.pop("L1_ffn_" + n) for n in ("W1", "b1", "W2", "b2"))
    pack = np.zeros((NX, P, NHX + D), np.float32)
    pack[:, 0:D, 0:NHX], pack[:, D, 0:NHX], pack[:, 96, 0:D], pack[:, :, NHX:] = w1, b1, b2, w2
    inputs["t_experts"] = pack
    for name, a in list(inputs.items()) + [(k, np.ascontiguousarray(v, dtype=np.float32)) for k, v in _constants().items()]:
        a = np.ascontiguousarray(a)
        arrays[f"in_{name}_dram"] = a
        t_in[name] = nc.dram_tensor(f"in_{name}_dram", a.shape, mybir.dt.from_np(a.dtype), kind="ExternalInput").ap()
    out = nc.dram_tensor("out_0_dram", (B, NTOK, D), F32, kind="ExternalOutput").ap()
    build(nc, t_in, out)
    r = run_bass_kernel_spmd(nc, [arrays], core_ids=[0])
    return r.results[0]["out_0_dram"]
```
